# Optimizing a Trainium2 kernel written in Bass

```python
import numpy as np
import jax
import jax.numpy as jnp

def _softmax(x, axis=-1):
    return jax.nn.softmax(x, axis=axis)

def _gelu(x):
    return jax.nn.gelu(x, approximate=True)

def _silu(x):
    return jax.nn.silu(x)

def _sigmoid(x):
    return jax.nn.sigmoid(x)

def _layernorm(x, axis=-1, eps=1e-05):
    m = jnp.mean(x, axis=axis, keepdims=True)
    v = jnp.var(x, axis=axis, keepdims=True)
    return (x - m) / jnp.sqrt(v + eps)

def _scatter_add(tgt, idx, src, axis=0):
    return tgt.at[idx].add(src)

def _segment_sum(src, seg, n):
    return jax.ops.segment_sum(src, seg, n)
kernel_name = 'mk_lm_tower_d1_tok_ids768_r4_e644d3'

def setup_inputs(seed: int=0):
    np.random.seed(seed)
    _w = jnp.asarray

    def _rec_inputs():
        import jax
        import jax.numpy as jnp
        _rk = jax.random.key(seed)
        x = jax.random.randint(jax.random.fold_in(_rk, 1), (8, 512), 0, 31993, jnp.int32)
        return x
    x = _rec_inputs()

    def _L0_tok_setup():
        import jax, jax.numpy as jnp
        import numpy as np
        VOCAB = 8000
        key = jax.random.key(seed)
        k1, k2 = jax.random.split(key)
        input_ids = jax.random.randint(k1, (4, 512), 0, VOCAB, dtype=jnp.int64 if jax.config.jax_enable_x64 else jnp.int32)
        weight = jax.random.normal(k2, (VOCAB, 192), dtype=jnp.float32)
        return {'input_ids': input_ids, 'weight': weight}
    _L0_tok_all = _L0_tok_setup()
    _L0_tok_in = {k: v for k, v in _L0_tok_all.items() if k in ('weight',)}
    del _L0_tok_all

    def _L0_attn_setup():
        import jax, jax.numpy as jnp
        import numpy as np
        EPS = 1e-05
        B, T, C = (8, 512, 192)
        H = 4 * C
        LAYER_ID, N_LAYER = (4, 12)

        def _ln(x, w, b):
            mu = x.mean(-1, keepdims=True)
            var = ((x - mu) ** 2).mean(-1, keepdims=True)
            return (x - mu) / jnp.sqrt(var + EPS) * w + b

        def _wkv_scan(w, k, v):
            a0 = jnp.zeros(k.shape[1:], k.dtype)
            b0 = jnp.zeros_like(a0)
            m0 = jnp.full_like(a0, -1e+38)

            def step(carry, kv):
                a, b, m = carry
                kt, vt = kv
                mm = jnp.maximum(m + w, kt)
                e1 = jnp.exp(m + w - mm)
                e2 = jnp.exp(kt - mm)
                return ((e1 * a + e2 * vt, e1 * b + e2, mm), (a, b, m))
            _, (A, Bd, M) = jax.lax.scan(step, (a0, b0, m0), (k, v))
            return (A, Bd, M)

        def bi_wkv(w, u, k, v):
            kt = jnp.swapaxes(k, 0, 1)
            vt = jnp.swapaxes(v, 0, 1)
            af, bf, mf = _wkv_scan(w, kt, vt)
            ab, bb, mb = _wkv_scan(w, kt[::-1], vt[::-1])
            ab, bb, mb = (ab[::-1], bb[::-1], mb[::-1])
            kk = kt + u
            M = jnp.maximum(jnp.maximum(mf, mb), kk)
            ef = jnp.exp(mf - M)
            eb = jnp.exp(mb - M)
            ec = jnp.exp(kk - M)
            y = (ef * af + eb * ab + ec * vt) / (ef * bf + eb * bb + ec)
            return jnp.swapaxes(y, 0, 1)
        key = jax.random.key(seed)
        ks = jax.random.split(key, 9)
        x = jax.random.normal(ks[0], (B, T, C), jnp.float32)
        r01 = LAYER_ID / (N_LAYER - 1)
        h = np.arange(C, dtype=np.float64)
        decay = (-5.0 + 8.0 * (h / (C - 1)) ** (0.7 + 1.3 * r01)).astype(np.float32)
        zigzag = ((np.arange(C) + 1) % 3 - 1).astype(np.float32) * 0.5
        first = (np.float32(np.log(0.3)) + zigzag).astype(np.float32)
        s = 0.02
        return {'x': x, 'ln1_w': jnp.ones((C,), jnp.float32), 'ln1_b': jnp.zeros((C,), jnp.float32), 'ln2_w': jnp.ones((C,), jnp.float32), 'ln2_b': jnp.zeros((C,), jnp.float32), 'decay': jnp.asarray(decay), 'first': jnp.asarray(first), 'Wk_a': s * jax.random.normal(ks[1], (C, C), jnp.float32), 'Wv_a': s * jax.random.normal(ks[2], (C, C), jnp.float32), 'Wr_a': s * jax.random.normal(ks[3], (C, C), jnp.float32), 'Wo_a': s * jax.random.normal(ks[4], (C, C), jnp.float32), 'Wk_f': s * jax.random.normal(ks[5], (H, C), jnp.float32), 'Wv_f': s * jax.random.normal(ks[6], (C, H), jnp.float32), 'Wr_f': s * jax.random.normal(ks[7], (C, C), jnp.float32)}
    _L0_attn_all = _L0_attn_setup()
    _L0_attn_in = {k: v for k, v in _L0_attn_all.items() if k in ('ln1_w', 'ln1_b', 'ln2_w', 'ln2_b', 'decay', 'first', 'Wk_a', 'Wv_a', 'Wr_a', 'Wo_a', 'Wk_f', 'Wv_f', 'Wr_f')}
    del _L0_attn_all

    def _L0_ffn_setup():
        import jax, jax.numpy as jnp
        import numpy as np
        B, S, D_IN, D_HID, D_OUT = (32, 128, 192, 768, 192)
        key = jax.random.key(seed)
        k1, k2, k3, k4 = jax.random.split(key, 4)
        init_k = float(np.sqrt(1.0 / D_IN))
        init_k2 = float(np.sqrt(1.0 / D_HID))
        x = jax.random.normal(k1, (B, S, D_IN), dtype=jnp.float32)
        in_weight = jax.random.uniform(k2, (D_HID, D_IN), dtype=jnp.float32, minval=-init_k, maxval=init_k)
        in_bias = jax.random.uniform(k3, (D_HID,), dtype=jnp.float32, minval=-init_k, maxval=init_k)
        out_weight = jax.random.uniform(k4, (D_HID, D_OUT), dtype=jnp.float32, minval=-init_k2, maxval=init_k2)
        return {'x': x, 'in_weight': in_weight, 'in_bias': in_bias, 'out_weight': out_weight}
    _L0_ffn_all = _L0_ffn_setup()
    _L0_ffn_in = {k: v for k, v in _L0_ffn_all.items() if k in ('in_weight', 'in_bias', 'out_weight')}
    del _L0_ffn_all
    return {'x': x, 'L0_tok_weight': _L0_tok_in['weight'], 'L0_attn_ln1_w': _L0_attn_in['ln1_w'], 'L0_attn_ln1_b': _L0_attn_in['ln1_b'], 'L0_attn_ln2_w': _L0_attn_in['ln2_w'], 'L0_attn_ln2_b': _L0_attn_in['ln2_b'], 'L0_attn_decay': _L0_attn_in['decay'], 'L0_attn_first': _L0_attn_in['first'], 'L0_attn_Wk_a': _L0_attn_in['Wk_a'], 'L0_attn_Wv_a': _L0_attn_in['Wv_a'], 'L0_attn_Wr_a': _L0_attn_in['Wr_a'], 'L0_attn_Wo_a': _L0_attn_in['Wo_a'], 'L0_attn_Wk_f': _L0_attn_in['Wk_f'], 'L0_attn_Wv_f': _L0_attn_in['Wv_f'], 'L0_attn_Wr_f': _L0_attn_in['Wr_f'], 'L0_ffn_in_weight': _L0_ffn_in['in_weight'], 'L0_ffn_in_bias': _L0_ffn_in['in_bias'], 'L0_ffn_out_weight': _L0_ffn_in['out_weight']}

def reference(x, L0_tok_weight, L0_attn_ln1_w, L0_attn_ln1_b, L0_attn_ln2_w, L0_attn_ln2_b, L0_attn_decay, L0_attn_first, L0_attn_Wk_a, L0_attn_Wv_a, L0_attn_Wr_a, L0_attn_Wo_a, L0_attn_Wk_f, L0_attn_Wv_f, L0_attn_Wr_f, L0_ffn_in_weight, L0_ffn_in_bias, L0_ffn_out_weight):
    import jax
    import jax.numpy as jnp

    def _L0_tok_ref(input_ids, weight):
        import jax, jax.numpy as jnp
        import numpy as np
        VOCAB = 8000
        one_hot = jax.nn.one_hot(input_ids, VOCAB, dtype=weight.dtype)
        return jnp.einsum('bsv,vd->bsd', one_hot, weight)

    def _L0_attn_ref(x, ln1_w, ln1_b, ln2_w, ln2_b, decay, first, Wk_a, Wv_a, Wr_a, Wo_a, Wk_f, Wv_f, Wr_f):
        import jax, jax.numpy as jnp
        import numpy as np
        EPS = 1e-05
        B, T, C = (8, 512, 192)
        H = 4 * C
        LAYER_ID, N_LAYER = (4, 12)

        def _ln(x, w, b):
            mu = x.mean(-1, keepdims=True)
            var = ((x - mu) ** 2).mean(-1, keepdims=True)
            return (x - mu) / jnp.sqrt(var + EPS) * w + b

        def _wkv_scan(w, k, v):
            a0 = jnp.zeros(k.shape[1:], k.dtype)
            b0 = jnp.zeros_like(a0)
            m0 = jnp.full_like(a0, -1e+38)

            def step(carry, kv):
                a, b, m = carry
                kt, vt = kv
                mm = jnp.maximum(m + w, kt)
                e1 = jnp.exp(m + w - mm)
                e2 = jnp.exp(kt - mm)
                return ((e1 * a + e2 * vt, e1 * b + e2, mm), (a, b, m))
            _, (A, Bd, M) = jax.lax.scan(step, (a0, b0, m0), (k, v))
            return (A, Bd, M)

        def bi_wkv(w, u, k, v):
            kt = jnp.swapaxes(k, 0, 1)
            vt = jnp.swapaxes(v, 0, 1)
            af, bf, mf = _wkv_scan(w, kt, vt)
            ab, bb, mb = _wkv_scan(w, kt[::-1], vt[::-1])
            ab, bb, mb = (ab[::-1], bb[::-1], mb[::-1])
            kk = kt + u
            M = jnp.maximum(jnp.maximum(mf, mb), kk)
            ef = jnp.exp(mf - M)
            eb = jnp.exp(mb - M)
            ec = jnp.exp(kk - M)
            y = (ef * af + eb * ab + ec * vt) / (ef * bf + eb * bb + ec)
            return jnp.swapaxes(y, 0, 1)
        Bn, Tn, Cn = x.shape
        h = _ln(x, ln1_w, ln1_b)
        k = h @ Wk_a.T
        v = h @ Wv_a.T
        sr = jax.nn.sigmoid(h @ Wr_a.T)
        y = bi_wkv(decay / Tn, first / Tn, k, v)
        x = x + sr * y @ Wo_a.T
        h = _ln(x, ln2_w, ln2_b)
        kf = jnp.square(jax.nn.relu(h @ Wk_f.T))
        x = x + jax.nn.sigmoid(h @ Wr_f.T) * (kf @ Wv_f.T)
        return x

    def _L0_ffn_ref(x, in_weight, in_bias, out_weight):
        import jax, jax.numpy as jnp
        import numpy as np
        B, S, D_IN, D_HID, D_OUT = (32, 128, 192, 768, 192)
        lead = x.shape[:-1]
        xt = x.reshape(-1, in_weight.shape[1])
        h = jax.nn.gelu(jnp.einsum('td,hd->th', xt, in_weight) + in_bias, approximate=False)
        out = jnp.einsum('th,ho->to', h, out_weight)
        return out.reshape(*lead, out_weight.shape[1])
    h = _L0_tok_ref(x, L0_tok_weight)
    h = h + _L0_attn_ref(_layernorm(h, axis=-1), L0_attn_ln1_w, L0_attn_ln1_b, L0_attn_ln2_w, L0_attn_ln2_b, L0_attn_decay, L0_attn_first, L0_attn_Wk_a, L0_attn_Wv_a, L0_attn_Wr_a, L0_attn_Wo_a, L0_attn_Wk_f, L0_attn_Wv_f, L0_attn_Wr_f)
    h = h + _L0_ffn_ref(_layernorm(h, axis=-1), L0_ffn_in_weight, L0_ffn_in_bias, L0_ffn_out_weight)
    return h

_drawn_inputs = setup_inputs


def setup_inputs(seed=0):
    import zlib

    import numpy as np

    out = dict(_drawn_inputs(seed))
    spreads = {'L0_attn_ln1_w': (1.0, 0.6),
     'L0_attn_ln1_b': (0.0, 0.1),
     'L0_attn_ln2_w': (1.0, 0.2),
     'L0_attn_ln2_b': (0.0, 0.29)}
    factors = {'L0_attn_first': 64.0,
     'L0_attn_Wr_a': 25.845,
     'L0_attn_Wr_f': 3.13,
     'L0_ffn_in_bias': 3.573}
    for name, (base, spread) in spreads.items():
        noise = np.random.default_rng([zlib.crc32(name.encode()), seed]).standard_normal(out[name].shape)
        drawn = base * np.exp(spread * noise) if base else spread * noise
        out[name] = jnp.asarray(drawn.astype(out[name].dtype))
    for name, factor in factors.items():
        out[name] = (out[name] * factor).astype(out[name].dtype)
    return out
```

```python
from contextlib import ExitStack

import concourse.bass as bass
from concourse import mybir

F32 = mybir.dt.float32
F32R = mybir.dt.float32r
I32 = mybir.dt.int32
U32 = mybir.dt.uint32
ALU = mybir.AluOpType
ACT = mybir.ActivationFunctionType

P = 128
EPS = 1e-5
M_START = -1e38


def tower(nc, x, table, ln1_w, ln1_b, ln2_w, ln2_b, decay, first, Wk, Wv, Wr, Wo, Wkf, Wvf, Wrf,
          w_in, b_in, w_out, out):
    B, T = x.shape
    VOCAB, C = table.shape
    HID = Wkf.shape[0]
    NT = T // P
    NH = HID // P
    CB = C - P
    PAIRS = B // 2
    assert T == 512 and P < C <= P + 64 and CB == 64 and HID % P == 0 and B % 2 == 0
    QKV = 5
    H0_SLOTS = 3

    steps = range(-2, PAIRS + 1)

    def has(p):
        return 0 <= p < PAIRS

    CHUNKS = {"qkv": QKV, "mix": NH + 2, "ffn": NH}
    norms = []
    for s in steps:
        for kind, p in (("qkv", s + 1), ("mix", s - 1), ("ffn", s - 1)):
            if has(p):
                norms += [(kind, p, 0), (kind, p, 1)]
    norm_no = {key: n for n, key in enumerate(norms)}
    chunks_to, n = [], 0
    for kind, _, _ in norms:
        n += CHUNKS[kind]
        chunks_to.append(n)

    def chunk_end(kind, p, q):
        return chunks_to[norm_no[kind, p, q]]

    def chunk_start(kind, p, q):
        return chunk_end(kind, p, q) - CHUNKS[kind]

    token_outs = [(k, p, q) for p in range(PAIRS)
                  for k, q in (("attn", 0), ("attn", 1), ("chan", 0), ("chan", 1), ("ffn", 0), ("ffn", 1))]
    out_no = {key: 2 * n for n, key in enumerate(token_outs)}

    with ExitStack() as ctx:
        def sb(name, shape, dt=F32):
            return ctx.enter_context(nc.sbuf_tensor(name, shape, dt))

        def sem(name):
            return ctx.enter_context(nc.semaphore(name))

        ident = sb("ident", [P, P])
        vec_rows = sb("vec_rows", [5 + NH, C])
        vec_cols = sb("vec_cols", [P, 2, 5])
        b_in_col = sb("b_in_col", [P, NH])
        wu = sb("wu", [P, 2, 2])
        bias_qkv = sb("bias_qkv", [P, QKV])
        bias_half = sb("bias_half", [P, QKV])
        bias_kf = sb("bias_kf", [P, NH])
        minus_half = sb("minus_half", [P, 2 * NT])
        qkv_w = sb("qkv_w", [P, 4, QKV * P], F32R)
        kf_w = sb("kf_w", [P, 4, HID], F32R)
        in_w = sb("in_w", [P, 4, HID], F32R)
        rf_w = sb("rf_w", [P, 4, C], F32R)
        rf_bias = sb("rf_bias", [P, C], F32R)
        rf_pick = sb("rf_pick", [P, P], F32R)
        wo_a = sb("wo_a", [P, C])
        wo_b = sb("wo_b", [P, 2, C])
        vf_w = sb("vf_w", [P, NH, C])
        out_w = sb("out_w", [P, NH, C])
        ids = sb("ids", [P, B, NT], I32)
        id_f = sb("id_f", [P, B, NT])
        id_ok = sb("id_ok", [P, B, NT])
        rows = sb("rows", [P, B * NT], U32)

        h0 = sb("h0", [P, H0_SLOTS, 2, NT, C])
        resid = sb("resid", [P, 2, NT, C])
        gate = sb("gate", [P, 2, NT, C])
        normed = sb("normed", [P, 2, NT, C])
        NE = len(norms)
        stats = sb("stats", [P, 2, NT, 6])
        mean_var = sb("mean_var", [P, NE, NT, 2])
        var_arg = sb("var_arg", [P, NE, 2, NT])
        rstd = sb("rstd", [P, NE, 2, NT])
        shift = sb("shift", [P, NE, 2, NT])

        act_a = sb("act_a", [P, 2, 2, T], F32R)
        act_b = sb("act_b", [P, 2, T], F32R)
        key = sb("key", [P, 2, 3, T])
        val = sb("val", [P, 2, 3, T])
        rec = sb("rec", [P, 2, 3, T])
        mx = sb("mx", [P, 2 * (T + 1)])
        ex = sb("ex", [P, 4, T])
        ev = sb("ev", [P, 2, T])
        st = sb("st", [P, 4, T])
        wt = sb("wt", [P, 2, 2, T])
        cen = sb("cen", [P, 2, 2, T])
        pos = sb("pos", [P, 2, T])
        hid = sb("hid", [P, 2, NH, T])

        nat_qkv = hid[:, 0, 0:2, :].rearrange("p a t -> p (a t)")[:, 0:QKV * C].rearrange("p (m c) -> p m c", c=C)
        nat_wo = hid[:, 0, 2, 0:2 * C].rearrange("p (m c) -> p m c", c=C)
        nat_rf = hid[:, 0, 3, 0:2 * C].rearrange("p (m c) -> p m c", c=C)
        nat_rf_t = hid[:, 0, 4, 0:2 * C].rearrange("p (m c) -> p m c", c=C)
        ln2b_rep = hid[:, 0, 5, 0:2 * P].rearrange("p (m c) -> p m c", c=P)
        rf_bias_h = hid[:, 0, 5, 2 * P:2 * P + C]
        nat_kf = hid[:, 1, 0:3, :].rearrange("p a t -> p (a t)")[:, 0:NH * C].rearrange("p (m c) -> p m c", c=C)
        nat_in = hid[:, 1, 3:6, :].rearrange("p a t -> p (a t)")[:, 0:NH * C].rearrange("p (m c) -> p m c", c=C)
        nat_vf = st[:, :, :].rearrange("p b t -> p (b t)")[:, 0:2 * HID].rearrange("p (m c) -> p m c", c=HID)
        ln1b_all = st[:, 3, 0:C]
        ln2b_all = st[:, 3, C:2 * C]
        junk = ev[:, 0, 0:C]

        ps_t = ctx.enter_context(nc.psum_tensor("ps_t", [P, 2, T], F32))
        ps_c = ctx.enter_context(nc.psum_tensor("ps_c", [P, 4, T], F32))
        ps_o = ctx.enter_context(nc.psum_tensor("ps_o", [P, 2, 512], F32))
        RING = 4

        ids_in = sem("ids_in")
        vecs_in = sem("vecs_in")
        lnb_in = sem("lnb_in")
        nat_qkv_in = sem("nat_qkv_in")
        nat_wo_in = sem("nat_wo_in")
        nat_rf_in = sem("nat_rf_in")
        nat_kf_in = sem("nat_kf_in")
        nat_in_in = sem("nat_in_in")
        nat_vf_in = sem("nat_vf_in")
        out_w_in = sem("out_w_in")
        gathered = [sem(f"gathered{b}") for b in range(B)]
        out_stored = [sem(f"out_stored{q}") for q in range(2)]
        consts = sem("consts")
        h0_cleared = sem("h0_cleared")
        rows_ready = sem("rows_ready")
        edges_ready = sem("edges_ready")
        prep_filled = sem("prep_filled")
        prep_high = sem("prep_high")
        prep_low = sem("prep_low")
        cols_ready = sem("cols_ready")
        bias_ready = sem("bias_ready")
        var_ready = sem("var_ready")
        rstd_ready = sem("rstd_ready")
        shift_ready = sem("shift_ready")
        normed_ready = sem("normed_ready")
        x0_ready = sem("x0_ready")
        res_ready = sem("res_ready")
        h1_ready = sem("h1_ready")
        t_filled = sem("t_filled")
        high_ready = sem("high_ready")
        low_ready = sem("low_ready")
        c_filled = sem("c_filled")
        c_freed = sem("c_freed")
        hid_ready = sem("hid_ready")
        o_filled = sem("o_filled")
        o_freed = sem("o_freed")
        d_ready = sem("d_ready")
        e_ready = sem("e_ready")
        ev_ready = sem("ev_ready")
        w_arg = sem("w_arg")
        w_ready = sem("w_ready")
        ecv_ready = sem("ecv_ready")
        st_ready = sem("st_ready")
        sw_ready = sem("sw_ready")
        sum_ready = sem("sum_ready")
        rden_ready = sem("rden_ready")
        z_ready = sem("z_ready")
        act_step = sem("act_step")
        dve_step = sem("dve_step")
        pool_step = sem("pool_step")
        pe_step = sem("pe_step")

        prep = []
        for m in range(0, QKV, 2):
            prep.append(("split", qkv_w, nat_qkv, m, [P] * min(2, QKV - m), 0))
        prep.append(("wo", None, nat_wo, 0, [P, CB], None))
        prep.append(("rf", rf_w, nat_rf, 0, [P, CB], 1))
        for m in range(0, NH, 2):
            prep.append(("split", kf_w, nat_kf, m, [P, P], 1))
        for m in range(0, NH, 2):
            prep.append(("vf", None, nat_vf, m, [P, P], None))
        for m in range(0, NH, 2):
            prep.append(("split", in_w, nat_in, m, [P, P], None))
        SPLIT_W = {id(qkv_w): nat_qkv_in, id(kf_w): nat_kf_in, id(in_w): nat_in_in}
        PREPS = len(prep) + 2

        def splits(k):
            return sum(item[0] in ("split", "rf") for item in prep[:k])

        block = ctx.enter_context(nc.Block())

        @block.sync
        def _(sp):
            sp.dma_start(ids[:], x.rearrange("b (p j) -> p b j", j=NT)).then_inc(ids_in, 16)
            for n, v in enumerate((ln1_w, ln2_w, decay, first, ln2_b)):
                sp.dma_start(vec_rows[n:n + 1, :], v.rearrange("(a c) -> a c", a=1)).then_inc(vecs_in, 16)
            sp.dma_start(vec_rows[5:5 + NH, 0:P], b_in.rearrange("(a c) -> a c", c=P)).then_inc(vecs_in, 16)
            for m, w in enumerate((Wk, Wv, Wr)):
                sp.dma_start(nat_qkv[:, m, :], w[0:P, :]).then_inc(nat_qkv_in, 16)
            for m, half, w in ((3, 0, Wk), (3, 1, Wv), (4, 0, Wr), (4, 1, Wr)):
                sp.dma_start(nat_qkv[64 * half:64 * half + 64, m, :], w[P:C, :]).then_inc(nat_qkv_in, 16)
            sp.dma_start(ln1b_all, ln1_b.partition_broadcast(P)).then_inc(lnb_in, 16)
            sp.dma_start(ln2b_all, ln2_b.partition_broadcast(P)).then_inc(lnb_in, 16)
            for w, nat, s in ((Wo, nat_wo, nat_wo_in), (Wrf, nat_rf, nat_rf_in)):
                sp.dma_start(nat[:, 0, :], w[0:P, :]).then_inc(s, 16)
                sp.dma_start(nat[0:CB, 1, :], w[P:C, :]).then_inc(s, 16)
            sp.dma_start(nat_kf, Wkf.rearrange("(m p) c -> p m c", p=P)).then_inc(nat_kf_in, 16)
            sp.dma_start(nat_vf[:, 0, :], Wvf[0:P, :]).then_inc(nat_vf_in, 16)
            sp.dma_start(nat_vf[0:CB, 1, :], Wvf[P:C, :]).then_inc(nat_vf_in, 16)
            sp.dma_start(nat_in, w_in.rearrange("(m p) c -> p m c", p=P)).then_inc(nat_in_in, 16)
            sp.dma_start(out_w[:], w_out.rearrange("(m p) c -> p m c", p=P)).then_inc(out_w_in, 16)
            for p in range(PAIRS):
                for q in range(2):
                    sp.wait_ge(o_freed, out_no["ffn", p, q] + 2)
                    sp.dma_start(out[2 * p + q].rearrange("(p j) c -> p (j c)", j=NT),
                                 resid[:, q].rearrange("p j c -> p (j c)")).then_inc(out_stored[q], 16)
            for q in range(2):
                sp.wait_ge(out_stored[q], 16 * PAIRS)

        @block.gpsimd
        def _(pool):
            g = nc.gpsimd
            g.memset(ident[:], 0.0).then_inc(pool_step, 1)
            pool.wait_ge(pool_step, 1)
            g.affine_select(out=ident[:], in_=ident[:], compare_op=ALU.not_equal, fill=1.0, base=0,
                            pattern=[[-1, P]], channel_multiplier=1).then_inc(consts, 1)
            g.memset(minus_half[:], -0.5).then_inc(consts, 1)

            def gather(p):
                if p >= H0_SLOTS:
                    pool.wait_ge(res_ready, 2 * (p - H0_SLOTS) + 2)
                g.memset(h0[:, p % H0_SLOTS], 0.0).then_inc(h0_cleared, 1)
                pool.wait_ge(h0_cleared, p + 1)
                if p == 0:
                    pool.wait_ge(rows_ready, 1)
                for q in range(2):
                    b = 2 * p + q
                    for j in range(NT):
                        g.indirect_dma_start(
                            out=h0[:, p % H0_SLOTS, q, j, :], out_offset=None, in_=table,
                            in_offset=bass.IndirectOffsetOnAxis(ap=rows[:, b * NT + j:b * NT + j + 1], axis=0),
                            bounds_check=VOCAB - 1, oob_is_err=False).then_inc(gathered[b], 16)

            def inv_sqrt(kind, p, q):
                e = norm_no[kind, p, q]
                k = 2 if kind == "qkv" else 1
                if e == 0:
                    pool.wait_ge(consts, 2)
                pool.wait_ge(var_ready, e + 1)
                g.tensor_tensor(rstd[:, e, 0:k, :].rearrange("p k j -> p (k j)"),
                                var_arg[:, e, 0:k, :].rearrange("p k j -> p (k j)"),
                                minus_half[:, 0:k * NT], ALU.pow).then_inc(rstd_ready, 1)

            def first_residual(p, q):
                e = norm_no["qkv", p, q]
                pool.wait_ge(shift_ready, e + 1)
                if p:
                    pool.wait_ge(out_stored[q], 16 * p)
                for j in range(NT):
                    ins = g.tensor_scalar(resid[:, q, j, :], h0[:, p % H0_SLOTS, q, j, :],
                                          rstd[:, e, 0, j:j + 1], shift[:, e, 0, j:j + 1], ALU.mult, ALU.add)
                ins.then_inc(x0_ready, 1)

            def second_residual(p, q):
                pool.wait_ge(normed_ready, norm_no["mix", p, q] + 1)
                r = resid[:, q].rearrange("p j c -> p (j c)")
                g.tensor_tensor(r, r, h0[:, p % H0_SLOTS, q].rearrange("p j c -> p (j c)"),
                                ALU.add).then_inc(res_ready, 1)

            def weigh_values(p, j):
                t = 3 * p + j
                pool.wait_ge(e_ready, 2 * t + 2)
                if t:
                    pool.wait_ge(st_ready, 4 * t)
                v = val[:, p % 2, j, :].unsqueeze(1).to_broadcast([P, 2, T])
                g.tensor_tensor(ev[:], ex[:, 2:4, :], v, ALU.mult).then_inc(ev_ready, 1)

            def weigh_centre(p, j):
                t = 3 * p + j
                pool.wait_ge(w_ready, 2 * t + 2)
                g.tensor_tensor(cen[:, t % 2, 0, :], cen[:, t % 2, 1, :], val[:, p % 2, j, :],
                                ALU.mult).then_inc(ecv_ready, 1)

            def weigh_states(p, j):
                t = 3 * p + j
                for n in range(2):
                    pool.wait_ge(st_ready, 4 * t + 2 * n + 2)
                    s = st[:, 2 * n:2 * n + 2, :]
                    g.tensor_tensor(s, s, wt[:, t % 2], ALU.mult).then_inc(sw_ready, 1)

            gather(0)
            for s in steps:
                mix, wkv, nxt = s - 1, s, s + 2
                if has(nxt) and 0 < nxt < H0_SLOTS:
                    gather(nxt)
                if has(mix):
                    first_residual(mix, 0)
                    first_residual(mix, 1)
                if has(wkv):
                    weigh_values(wkv, 0)
                    weigh_centre(wkv, 0)
                if has(mix):
                    inv_sqrt("mix", mix, 0)
                    inv_sqrt("mix", mix, 1)
                if has(wkv):
                    weigh_states(wkv, 0)
                if has(mix):
                    second_residual(mix, 0)
                    second_residual(mix, 1)
                if has(nxt) and nxt >= H0_SLOTS:
                    gather(nxt)
                if has(wkv):
                    for j in (1, 2):
                        weigh_values(wkv, j)
                        weigh_centre(wkv, j)
                        weigh_states(wkv, j)
                if has(mix):
                    inv_sqrt("ffn", mix, 0)
                    inv_sqrt("ffn", mix, 1)
                if has(nxt):
                    inv_sqrt("qkv", nxt, 0)
                    inv_sqrt("qkv", nxt, 1)

        @block.scalar
        def _(act):
            a = nc.scalar
            own = [0]

            def after(ins):
                own[0] += 1
                ins.then_inc(act_step, 1)
                act.wait_ge(act_step, own[0])

            def prepare(first_item, last_item):
                for n, (kind, dst, nat, m, sizes, ln) in list(enumerate(prep))[first_item:last_item]:
                    bank = ps_c[:, (n + 1) % RING]
                    if n == first_item and first_item == 0:
                        act.wait_ge(cols_ready, 5)
                    act.wait_ge(prep_filled, n + 2)
                    cols = sum(sizes)
                    if kind == "split" or kind == "rf":
                        if kind == "rf":
                            a.activation(nat_rf_t[:, 0, :], bank[:, 0:C], ACT.Identity).then_inc(act_step, 1)
                            a.activation(nat_rf_t[:, 1, :], bank[:, 256:256 + C], ACT.Identity).then_inc(act_step, 1)
                            own[0] += 2
                        at = m * P
                        sa = 1.0 if ln is None else vec_cols[:, 0, ln:ln + 1]
                        sb_ = 1.0 if ln is None else vec_cols[64:128, 1, ln:ln + 1]
                        a.activation(dst[:, 0, at:at + cols], bank[:, 0:cols], ACT.Identity, scale=sa)\
                            .then_inc(act_step, 1)
                        a.activation(dst[64:128, 2, at:at + cols], bank[64:128, 256:256 + cols],
                                     ACT.Identity, scale=sb_).then_inc(act_step, 1)
                        own[0] += 2
                        a.activation(dst[0:64, 2, at:at + cols], bank[64:128, 256:256 + cols],
                                     ACT.Identity, scale=sb_).then_inc(prep_high, 1)
                    elif kind == "wo":
                        a.activation(wo_a[:], bank[:, 0:C], ACT.Identity, scale=0.5).then_inc(act_step, 1)
                        own[0] += 1
                        act.wait_ge(edges_ready, 3)
                        a.activation(wo_b[0:64, 0, :], bank[64:128, 256:256 + C], ACT.Identity, scale=0.5)\
                            .then_inc(act_step, 1)
                        own[0] += 1
                        a.activation(wo_b[64:128, 1, :], bank[64:128, 256:256 + C], ACT.Identity, scale=0.5)\
                            .then_inc(prep_high, 1)
                    else:
                        a.activation(vf_w[:, m:m + 2, :], bank[:, 0:2 * C].rearrange("p (m c) -> p m c", c=C),
                                     ACT.Identity, scale=0.5).then_inc(prep_high, 1)

            def round_high(kind, p, q):
                e = norm_no[kind, p, q]
                act.wait_ge(t_filled, e + 1)
                if e >= 2:
                    act.wait_ge(c_filled, chunks_to[e - 2])
                a.activation(act_a[:, e % 2, 0, :], ps_t[:, 0], ACT.Identity).then_inc(high_ready, 1)
                a.activation(act_b[64:128, e % 2, :], ps_t[64:128, 1], ACT.Identity).then_inc(high_ready, 1)

            def take_qkv(p, q):
                n, slot = chunk_start("qkv", p, q), p % 2
                if p >= 2:
                    act.wait_ge(z_ready, 3 * (p - 1))
                    act.wait_ge(o_filled, out_no["attn", p - 2, 1] + 2)
                bank = [ps_c[:, (n + i) % RING] for i in range(QKV)]
                act.wait_ge(c_filled, n + 1)
                if n == 0:
                    act.wait_ge(bias_ready, 1)
                a.activation(key[:, slot, q, :], bank[0], ACT.Identity, bias=bias_qkv[:, 0:1]).then_inc(c_freed, 1)
                act.wait_ge(c_filled, n + 2)
                a.activation(val[:, slot, q, :], bank[1], ACT.Identity, bias=bias_qkv[:, 1:2]).then_inc(c_freed, 1)
                act.wait_ge(c_filled, n + 3)
                a.activation(rec[:, slot, q, :], bank[2], ACT.Tanh, bias=bias_half[:, 2:3], scale=0.5)\
                    .then_inc(c_freed, 1)
                act.wait_ge(c_filled, n + 4)
                mine = slice(64 * q, 64 * q + 64)
                own[0] += 1
                a.activation(key[mine, slot, 2, :], bank[3][0:64], ACT.Identity, bias=bias_qkv[0:64, 3:4])\
                    .then_inc(act_step, 1)
                a.activation(val[mine, slot, 2, :], bank[3][64:128], ACT.Identity, bias=bias_qkv[64:128, 3:4])\
                    .then_inc(c_freed, 1)
                act.wait_ge(c_filled, n + 5)
                a.activation(rec[mine, slot, 2, :], bank[4][mine], ACT.Tanh, bias=bias_half[mine, 4:5], scale=0.5)\
                    .then_inc(c_freed, 1)

            def exp_steps(p, j):
                t, part = 3 * p + j, j // 2
                act.wait_ge(d_ready, 2 * t + 1)
                a.activation(ex[:, 0:2, :], ex[:, 0:2, :], ACT.Exp, bias=wu[:, part, 0:1]).then_inc(e_ready, 1)
                act.wait_ge(d_ready, 2 * t + 2)
                a.activation(ex[:, 2:4, :], ex[:, 2:4, :], ACT.Exp).then_inc(e_ready, 1)

            def exp_weights(p, j):
                t, part = 3 * p + j, j // 2
                act.wait_ge(w_arg, 2 * t + 1)
                a.activation(wt[:, t % 2], wt[:, t % 2], ACT.Exp).then_inc(w_ready, 1)
                act.wait_ge(w_arg, 2 * t + 2)
                a.activation(cen[:, t % 2, 1, :], cen[:, t % 2, 1, :], ACT.Exp, bias=wu[:, part, 1:2])\
                    .then_inc(w_ready, 1)

            def invert(p, j):
                t = 3 * p + j
                act.wait_ge(sum_ready, t + 1)
                d = wt[:, t % 2, 1, :]
                after(a.activation(d, d, ACT.Ln))
                a.activation(d, d, ACT.Exp, scale=-1.0).then_inc(rden_ready, 1)

            def take_mix(p, q):
                n = chunk_start("mix", p, q)
                b = 2 * p + q
                if p:
                    act.wait_ge(o_filled, out_no["ffn", p - 1, q] + 2)
                for m in range(NH):
                    act.wait_ge(c_filled, n + m + 1)
                    a.activation(pos[:, m % 2, :], ps_c[:, (n + m) % RING], ACT.Relu, bias=bias_kf[:, m:m + 1])\
                        .then_inc(c_freed, 1)
                    act.wait_ge(c_freed, n + m + 1)
                    a.activation(hid[:, q, m, :], pos[:, m % 2, :], ACT.Square).then_inc(hid_ready, 1)
                if p:
                    act.wait_ge(h1_ready, b - 1)
                for h in range(2):
                    act.wait_ge(c_filled, n + NH + h + 1)
                    a.activation(gate[:, q, 2 * h:2 * h + 2, :].rearrange("p j c -> p (j c)"),
                                 ps_c[:, (n + NH + h) % RING, 0:2 * C], ACT.Tanh, scale=0.5).then_inc(c_freed, 1)

            def take_ffn(p, q):
                n = chunk_start("ffn", p, q)
                act.wait_ge(o_filled, out_no["chan", p, q] + 2)
                for m in range(NH):
                    act.wait_ge(c_filled, n + m + 1)
                    a.activation(hid[:, q, m, :], ps_c[:, (n + m) % RING], ACT.Gelu, bias=b_in_col[:, m:m + 1])\
                        .then_inc(c_freed, 1)

            prepare(0, 3)
            for s in steps:
                mix, wkv, prj = s - 1, s, s + 1
                if has(prj):
                    round_high("qkv", prj, 0)
                if s == -1:
                    round_high("qkv", prj, 1)
                    take_qkv(prj, 0)
                    take_qkv(prj, 1)
                    prepare(3, len(prep))
                    act.wait_ge(prep_filled, PREPS)
                    bank = ps_c[:, (PREPS - 1) % RING]
                    act.wait_ge(edges_ready, 3)
                    a.activation(rf_bias[0:1, :], bank[0:1, 0:C], ACT.Identity).then_inc(act_step, 1)
                    own[0] += 1
                    a.activation(rf_bias_h[32:33, :].bitcast(F32R), bank[32:33, 0:C], ACT.Identity)\
                        .then_inc(prep_high, 1)
                    continue
                if has(wkv):
                    exp_steps(wkv, 0)
                if has(prj):
                    round_high("qkv", prj, 1)
                if has(wkv):
                    exp_weights(wkv, 0)
                if has(prj):
                    take_qkv(prj, 0)
                if has(mix):
                    round_high("mix", mix, 0)
                if has(wkv):
                    invert(wkv, 0)
                if has(prj):
                    take_qkv(prj, 1)
                if has(mix):
                    round_high("mix", mix, 1)
                if has(wkv):
                    exp_steps(wkv, 1)
                    exp_weights(wkv, 1)
                if has(mix):
                    take_mix(mix, 0)
                if has(wkv):
                    invert(wkv, 1)
                    exp_steps(wkv, 2)
                    exp_weights(wkv, 2)
                if has(mix):
                    take_mix(mix, 1)
                if has(wkv):
                    invert(wkv, 2)
                if has(mix):
                    round_high("ffn", mix, 0)
                    take_ffn(mix, 0)
                    round_high("ffn", mix, 1)
                    take_ffn(mix, 1)

        @block.vector
        def _(dve):
            v = nc.vector
            own = [0]

            def step(ins):
                own[0] += 1
                ins.then_inc(dve_step, 1)
                return own[0]

            def after(ins):
                dve.wait_ge(dve_step, step(ins))

            def set_up():
                dve.wait_ge(ids_in, 16)
                after(v.tensor_scalar(id_ok[:], ids[:], 0.0, None, ALU.is_ge))
                after(v.scalar_tensor_tensor(id_ok[:], ids[:], float(VOCAB), id_ok[:], ALU.is_lt, ALU.mult))
                after(v.scalar_tensor_tensor(id_f[:], ids[:], -float(VOCAB), id_ok[:], ALU.add, ALU.mult))
                v.tensor_scalar(rows[:], id_f[:].rearrange("p b j -> p (b j)"), float(VOCAB), None, ALU.add)\
                    .then_inc(rows_ready, 1)
                dve.wait_ge(prep_filled, 1)
                bank = ps_c[:, 0]
                v.tensor_copy(vec_cols[:, 0, :], bank[:, 0:5]).then_inc(cols_ready, 1)
                v.tensor_copy(vec_cols[64:128, 1, :], bank[64:128, 16:21]).then_inc(cols_ready, 1)
                v.tensor_copy(vec_cols[0:64, 1, :], bank[64:128, 16:21]).then_inc(cols_ready, 1)
                v.tensor_copy(b_in_col[:], bank[:, 5:5 + NH]).then_inc(cols_ready, 1)
                dve.wait_ge(cols_ready, 4)
                v.tensor_scalar(wu[:], vec_cols[:, :, 2:4], 1.0 / T, None, ALU.mult).then_inc(cols_ready, 1)

            def set_edges():
                step(v.memset(mx[:, 0:1], M_START))
                step(v.memset(mx[:, 2 * T + 1:2 * T + 2], M_START))
                v.memset(wo_b[:], 0.0).then_inc(edges_ready, 1)
                v.memset(rf_bias[:].bitcast(F32), 0.0).then_inc(edges_ready, 1)
                v.memset(rf_pick[:].bitcast(F32), 0.0).then_inc(edges_ready, 1)
                dve.wait_ge(edges_ready, 3)
                step(v.memset(rf_pick[0:1, :].bitcast(F32), 1.0))
                step(v.memset(rf_pick[32:33, :].bitcast(F32), 1.0))

            def fold_bias(bias, w, lnb, m):
                after(v.scalar_tensor_tensor(junk, w[:, m, :], 1.0, lnb, ALU.mult, ALU.mult,
                                             accum_out=bias[:, m:m + 1]))

            def prepare(first_item, last_item):
                for n, (kind, dst, nat, m, sizes, ln) in list(enumerate(prep))[first_item:last_item]:
                    bank = ps_c[:, (n + 1) % RING]
                    dve.wait_ge(prep_high, n + 1)
                    if kind not in ("split", "rf"):
                        continue
                    cols, at = sum(sizes), m * P
                    sa = 1.0 if ln is None else vec_cols[:, 0, ln:ln + 1]
                    sb_ = 1.0 if ln is None else vec_cols[64:128, 1, ln:ln + 1]
                    step(v.scalar_tensor_tensor(dst[:, 1, at:at + cols], bank[:, 0:cols], sa,
                                                dst[:, 0, at:at + cols].bitcast(F32), ALU.mult, ALU.subtract))
                    for half in (1, 0):
                        ins = v.scalar_tensor_tensor(dst[64 * half:64 * half + 64, 3, at:at + cols],
                                                     bank[64:128, 256:256 + cols], sb_,
                                                     dst[64:128, 2, at:at + cols].bitcast(F32),
                                                     ALU.mult, ALU.subtract)
                        if half:
                            step(ins)
                    ins.then_inc(prep_low, 1)

            def statistics(kind, p, q, src):
                e = norm_no[kind, p, q]
                for j in range(NT):
                    done = step(v.bn_stats(stats[:, e % 2, j, :], src[:, j, :]))
                for j in range(NT):
                    dve.wait_ge(dve_step, done - NT + 1 + j)
                    last = step(v.bn_aggr(mean_var[:, e, j, :], stats[:, e % 2, j, :]))
                dve.wait_ge(dve_step, last)
                var = mean_var[:, e, :, 1]
                if kind == "qkv":
                    step(v.tensor_scalar(var_arg[:, e, 1, :], var, 1.0 + EPS, EPS * EPS, ALU.mult, ALU.add))
                v.tensor_scalar(var_arg[:, e, 0, :], var, EPS, None, ALU.add).then_inc(var_ready, 1)

            def normalise(kind, p, q, src):
                e = norm_no[kind, p, q]
                k = 2 if kind == "qkv" else 1
                dve.wait_ge(rstd_ready, e + 1)
                mean = mean_var[:, e, :, 0].unsqueeze(1).to_broadcast([P, k, NT])
                v.scalar_tensor_tensor(shift[:, e, 0:k, :], mean, -1.0, rstd[:, e, 0:k, :],
                                       ALU.mult, ALU.mult).then_inc(shift_ready, 1)
                dve.wait_ge(shift_ready, e + 1)
                if e >= 2:
                    dve.wait_ge(t_filled, e - 1)
                for j in range(NT):
                    ins = v.tensor_scalar(normed[:, e % 2, j, :], src[:, j, :], rstd[:, e, k - 1, j:j + 1],
                                          shift[:, e, k - 1, j:j + 1], ALU.mult, ALU.add)
                    if j < NT - 1:
                        step(ins)
                ins.then_inc(normed_ready, 1)

            def embed_statistics(p, q):
                dve.wait_ge(gathered[2 * p + q], 16 * NT)
                statistics("qkv", p, q, h0[:, p % H0_SLOTS, q])

            def embed_normalise(p, q):
                normalise("qkv", p, q, h0[:, p % H0_SLOTS, q])

            def split_low(kind, p, q):
                e = norm_no[kind, p, q]
                dve.wait_ge(high_ready, 2 * e + 1)
                v.tensor_tensor(act_a[:, e % 2, 1, :], ps_t[:, 0], act_a[:, e % 2, 0, :].bitcast(F32),
                                ALU.subtract).then_inc(low_ready, 1)
                dve.wait_ge(high_ready, 2 * e + 2)
                v.tensor_tensor(act_b[0:64, e % 2, :], ps_t[64:128, 1], act_b[64:128, e % 2, :].bitcast(F32),
                                ALU.subtract).then_inc(low_ready, 1)

            mx_excl = bass.AP(mx, 0, [[2 * (T + 1), P], [T + 2, 2], [1, T]])
            mx_incl = bass.AP(mx, 1, [[2 * (T + 1), P], [T, 2], [1, T]])
            mx_b = mx[:, T + 1:2 * T + 2]

            def maxima(p, j):
                t, part, k = 3 * p + j, j // 2, key[:, p % 2, j, :]
                w = wu[:, part, 0:1].to_broadcast([P, T])
                dve.wait_ge(c_freed, chunk_end("qkv", p, 1 if j else 0))
                if t:
                    dve.wait_ge(w_arg, 2 * t - 1)
                step(v.tensor_tensor_scan(mx[:, 1:T + 1], w, k, M_START, ALU.add, ALU.max))
                done = step(v.tensor_tensor_scan(bass.AP(mx, 2 * T, [[2 * (T + 1), P], [-1, T]]),
                                                 w, bass.AP(key, ((p % 2) * 3 + j) * T + T - 1, [[6 * T, P], [-1, T]]),
                                                 M_START, ALU.add, ALU.max))
                dve.wait_ge(dve_step, done)
                v.tensor_tensor(ex[:, 0:2, :], mx_excl, mx_incl, ALU.subtract).then_inc(d_ready, 1)
                v.tensor_tensor(ex[:, 2:4, :], k.unsqueeze(1).to_broadcast([P, 2, T]), mx_incl, ALU.subtract)\
                    .then_inc(d_ready, 1)

            def common_max(p, j):
                t, part, k = 3 * p + j, j // 2, key[:, p % 2, j, :]
                m = cen[:, t % 2, 0, :]
                after(v.tensor_tensor(m, mx[:, 0:T], mx_b[:, 1:T + 1], ALU.max))
                after(v.scalar_tensor_tensor(m, k, wu[:, part, 1:2], m, ALU.add, ALU.max))
                v.tensor_tensor(wt[:, t % 2], mx_excl, m.unsqueeze(1).to_broadcast([P, 2, T]), ALU.subtract)\
                    .then_inc(w_arg, 1)
                v.tensor_tensor(cen[:, t % 2, 1, :], k, m, ALU.subtract).then_inc(w_arg, 1)

            def back(tile, offset, count):
                return bass.AP(tile[:].tensor, offset, [[tile[:].ap[0][0], P], [-1, count]])

            def scans(p, j):
                t = 3 * p + j
                for n, (data, base) in enumerate(((ev, 0), (ex, 2 * T))):
                    if n == 0:
                        dve.wait_ge(ev_ready, t + 1)
                    src = ev[:, 0, :] if n == 0 else ex[:, 2, :]
                    v.tensor_tensor_scan(st[:, 2 * n, 1:T], ex[:, 0, 0:T - 1], src[:, 0:T - 1], 0.0,
                                         ALU.mult, ALU.add).then_inc(st_ready, 1)
                    v.tensor_tensor_scan(back(st, (2 * n + 1) * T + T - 2, T - 1),
                                         back(ex, T + T - 1, T - 1), back(data, base + T + T - 1, T - 1), 0.0,
                                         ALU.mult, ALU.add).then_inc(st_ready, 1)

            def sums(p, j):
                t = 3 * p + j
                dve.wait_ge(sw_ready, 2 * t + 2)
                dve.wait_ge(ecv_ready, t + 1)
                s = st[:].rearrange("p (n d) t -> p n d t", d=2)
                after(v.tensor_tensor(wt[:, t % 2], s[:, :, 0, :], s[:, :, 1, :], ALU.add))
                v.tensor_tensor(wt[:, t % 2], wt[:, t % 2], cen[:, t % 2], ALU.add).then_inc(sum_ready, 1)

            def gated(p, j):
                t = 3 * p + j
                dve.wait_ge(rden_ready, t + 1)
                y, r = wt[:, t % 2, 0, :], rec[:, p % 2, j, :]
                after(v.tensor_tensor(y, y, wt[:, t % 2, 1, :], ALU.mult))
                v.scalar_tensor_tensor(r, r, 1.0, y, ALU.add, ALU.mult).then_inc(z_ready, 1)

            def add_attention(p, q):
                n = out_no["attn", p, q]
                dve.wait_ge(x0_ready, 2 * p + q + 1)
                for h in range(2):
                    dve.wait_ge(o_filled, n + h + 1)
                    r = resid[:, q, 2 * h:2 * h + 2, :].rearrange("p j c -> p (j c)")
                    v.tensor_tensor(r, ps_o[:, h, 0:2 * C], r, ALU.add).then_inc(o_freed, 1)
                dve.wait_ge(o_freed, n + 2)
                statistics("mix", p, q, resid[:, q])

            def add_channel_mix(p, q):
                n = out_no["chan", p, q]
                dve.wait_ge(c_freed, chunk_end("mix", p, q))
                for h in range(2):
                    dve.wait_ge(o_filled, n + h + 1)
                    g = gate[:, q, 2 * h:2 * h + 2, :].rearrange("p j c -> p (j c)")
                    v.scalar_tensor_tensor(g, g, 1.0, ps_o[:, h, 0:2 * C], ALU.add, ALU.mult).then_inc(o_freed, 1)
                dve.wait_ge(o_freed, n + 2)
                dve.wait_ge(res_ready, 2 * p + q + 1)
                r = resid[:, q].rearrange("p j c -> p (j c)")
                v.tensor_tensor(r, r, gate[:, q].rearrange("p j c -> p (j c)"), ALU.add).then_inc(h1_ready, 1)
                dve.wait_ge(h1_ready, 2 * p + q + 1)
                statistics("ffn", p, q, resid[:, q])

            def add_ffn(p, q):
                n = out_no["ffn", p, q]
                for h in range(2):
                    dve.wait_ge(o_filled, n + h + 1)
                    r = resid[:, q, 2 * h:2 * h + 2, :].rearrange("p j c -> p (j c)")
                    v.tensor_tensor(r, ps_o[:, h, 0:2 * C], r, ALU.add).then_inc(o_freed, 1)

            set_up()
            set_edges()
            dve.wait_ge(lnb_in, 32)
            dve.wait_ge(nat_qkv_in, 16 * 7)
            for m in range(QKV):
                fold_bias(bias_qkv, nat_qkv, ln1b_all, m)
            v.tensor_scalar(bias_half[:], bias_qkv[:], 0.5, None, ALU.mult).then_inc(bias_ready, 1)
            prepare(0, 3)
            for s in steps:
                mix, wkv, prj, nxt = s - 1, s, s + 1, s + 2
                if has(prj):
                    split_low("qkv", prj, 0)
                if has(wkv):
                    maxima(wkv, 0)
                if has(prj):
                    split_low("qkv", prj, 1)
                if s == -1:
                    dve.wait_ge(nat_kf_in, 16)
                    for m in range(NH):
                        fold_bias(bias_kf, nat_kf, ln2b_all, m)
                    step(v.tensor_copy(ln2b_rep[:, 0, :], vec_cols[:, 0, 4:5].to_broadcast([P, P])))
                    step(v.memset(ln2b_rep[0:64, 1, :], 0.0))
                    v.tensor_copy(ln2b_rep[64:128, 1, :], vec_cols[64:128, 1, 4:5].to_broadcast([64, P]))\
                        .then_inc(bias_ready, 1)
                    prepare(3, len(prep))
                    dve.wait_ge(prep_high, len(prep) + 1)
                    v.tensor_tensor(rf_bias[32:33, :], ps_c[32:33, (PREPS - 1) % RING, 0:C],
                                    rf_bias_h[32:33, :], ALU.subtract).then_inc(prep_low, 1)
                    for n, edge in ((0, 0), (1, T - 1), (2, 0), (3, T - 1)):
                        step(v.memset(st[:, n, edge:edge + 1], 0.0))
                if has(wkv):
                    common_max(wkv, 0)
                if has(mix):
                    add_attention(mix, 0)
                    add_attention(mix, 1)
                    normalise("mix", mix, 0, resid[:, 0])
                    normalise("mix", mix, 1, resid[:, 1])
                if has(wkv):
                    scans(wkv, 0)
                if has(mix):
                    split_low("mix", mix, 0)
                if has(wkv):
                    maxima(wkv, 1)
                    sums(wkv, 0)
                if has(mix):
                    split_low("mix", mix, 1)
                if has(wkv):
                    common_max(wkv, 1)
                    gated(wkv, 0)
                    scans(wkv, 1)
                    maxima(wkv, 2)
                    sums(wkv, 1)
                    common_max(wkv, 2)
                    gated(wkv, 1)
                    scans(wkv, 2)
                if has(mix):
                    add_channel_mix(mix, 0)
                if has(wkv):
                    sums(wkv, 2)
                if has(mix):
                    normalise("ffn", mix, 0, resid[:, 0])
                    add_channel_mix(mix, 1)
                if has(wkv):
                    gated(wkv, 2)
                if has(mix):
                    normalise("ffn", mix, 1, resid[:, 1])
                    split_low("ffn", mix, 0)
                if has(nxt):
                    embed_statistics(nxt, 0)
                    embed_statistics(nxt, 1)
                if has(mix):
                    split_low("ffn", mix, 1)
                if has(nxt):
                    embed_normalise(nxt, 0)
                    embed_normalise(nxt, 1)
                if has(mix):
                    add_ffn(mix, 0)
                    add_ffn(mix, 1)

        @block.tensor
        def _(pe):
            mm = nc.tensor.matmul

            def turn(dst, src, rows_in):
                return nc.tensor.transpose(dst, src, ident[0:rows_in, 0:rows_in])

            def prepare(first_item, last_item):
                for n, (kind, dst, nat, m, sizes, ln) in list(enumerate(prep))[first_item:last_item]:
                    bank = ps_c[:, (n + 1) % RING]
                    if kind == "split":
                        sem_in = SPLIT_W[id(dst)]
                        pe.wait_ge(sem_in, 16 * 7 if sem_in is nat_qkv_in else 16)
                    else:
                        pe.wait_ge({"wo": nat_wo_in, "rf": nat_rf_in, "vf": nat_vf_in}[kind], 32)
                    if n >= RING:
                        pe.wait_ge(prep_high, n + 1 - RING)
                        pe.wait_ge(prep_low, splits(n + 1 - RING))
                    at = 0
                    if kind == "vf":
                        for i in range(2):
                            c = slice((m + i) * P, (m + i + 1) * P)
                            turn(bank[:, i * C:i * C + P], nat[:, 0, c], P)
                            ins = turn(bank[:, i * C + P:i * C + C], nat[0:CB, 1, c], CB)
                    else:
                        for i, size in enumerate(sizes):
                            turn(bank[:, at:at + size], nat[0:size, m + i, 0:P], size)
                            ins = turn(bank[:, 256 + at:256 + at + size], nat[0:size, m + i, C - P:C], size)
                            at += size
                    ins.then_inc(prep_filled, 1)

            def transposes(kind, p, q):
                e = norm_no[kind, p, q]
                pe.wait_ge(normed_ready, e + 1)
                if e:
                    pe.wait_ge(low_ready, 2 * e)
                for j in range(NT):
                    cols = slice(j, T, NT) if kind == "qkv" else slice(j * P, (j + 1) * P)
                    turn(ps_t[:, 0, cols], normed[:, e % 2, j, 0:P], P)
                    ins = turn(ps_t[:, 1, cols], normed[:, e % 2, j, C - P:C], P)
                ins.then_inc(t_filled, 1)

            def project(kind, p, q, w, chunks):
                e = norm_no[kind, p, q]
                n = chunk_start(kind, p, q)
                pe.wait_ge(low_ready, 2 * e + 2)
                high, low, b = act_a[:, e % 2, 0, :], act_a[:, e % 2, 1, :], act_b[:, e % 2, :]
                for m in range(chunks):
                    if n + m >= RING:
                        pe.wait_ge(c_freed, n + m + 1 - RING)
                    o, c = ps_c[:, (n + m) % RING], slice(m * P, (m + 1) * P)
                    mm(o, w[:, 0, c], high, start=True, stop=False)
                    mm(o, w[:, 1, c], high, start=False, stop=False)
                    mm(o, w[:, 0, c], low, start=False, stop=False)
                    mm(o, w[:, 2, c], b, start=False, stop=False)
                    mm(o, w[:, 3, c], b, start=False, stop=True).then_inc(c_filled, 1)

            def gate_rows(p, q):
                e = norm_no["mix", p, q]
                n = chunk_start("mix", p, q) + NH
                for h in range(2):
                    pe.wait_ge(c_freed, n + h + 1 - RING)
                    for i in range(2):
                        tok = slice((2 * h + i) * P, (2 * h + i + 1) * P)
                        o = ps_c[:, (n + h) % RING, i * C:(i + 1) * C]
                        high, low, b = act_a[:, e % 2, 0, tok], act_a[:, e % 2, 1, tok], act_b[:, e % 2, tok]
                        mm(o, high, rf_w[:, 0, :], start=True, stop=False)
                        mm(o, high, rf_w[:, 1, :], start=False, stop=False)
                        mm(o, low, rf_w[:, 0, :], start=False, stop=False)
                        mm(o, b, rf_w[:, 2, :], start=False, stop=False)
                        mm(o, b, rf_w[:, 3, :], start=False, stop=False)
                        ins = mm(o, rf_pick[:], rf_bias[:], start=False, stop=True)
                    ins.then_inc(c_filled, 1)

            def attention_out(p, q):
                n = out_no["attn", p, q]
                pe.wait_ge(z_ready, 3 * p + 3)
                for h in range(2):
                    if n + h >= 2:
                        pe.wait_ge(o_freed, n + h - 1)
                    for i in range(2):
                        o, tok = ps_o[:, h, i * C:(i + 1) * C], slice(2 * h + i, T, NT)
                        mm(o, rec[:, p % 2, q, tok], wo_a[:], start=True, stop=False)
                        ins = mm(o, rec[:, p % 2, 2, tok], wo_b[:, q, :], start=False, stop=True)
                    ins.then_inc(o_filled, 1)

            def hidden_out(kind, p, q, w):
                n = out_no[kind, p, q]
                for h in range(2):
                    pe.wait_ge(o_freed, n + h - 1)
                    for i in range(2):
                        o, j = ps_o[:, h, i * C:(i + 1) * C], 2 * h + i
                        for m in range(NH):
                            ins = mm(o, hid[:, q, m, j * P:(j + 1) * P], w[:, m, :],
                                     start=(m == 0), stop=(m == NH - 1))
                    ins.then_inc(o_filled, 1)

            def channel_out(p, q):
                pe.wait_ge(hid_ready, NH * (2 * p + q + 1))
                hidden_out("chan", p, q, vf_w)

            def ffn_out(p, q):
                pe.wait_ge(c_freed, chunk_end("ffn", p, q))
                hidden_out("ffn", p, q, out_w)

            pe.wait_ge(consts, 1)
            pe.wait_ge(vecs_in, 16 * 6)
            turn(ps_c[:, 0, 0:5 + NH], vec_rows[:, 0:P], 5 + NH)
            turn(ps_c[:, 0, 16:21], vec_rows[0:5, C - P:C], 5).then_inc(prep_filled, 1)
            prepare(0, 3)
            for s in steps:
                mix, prj = s - 1, s + 1
                if s == -1:
                    transposes("qkv", prj, 0)
                    transposes("qkv", prj, 1)
                    pe.wait_ge(prep_low, 3)
                    project("qkv", prj, 0, qkv_w, QKV)
                    project("qkv", prj, 1, qkv_w, QKV)
                    pe.wait_ge(c_freed, 2 * QKV)
                    prepare(3, len(prep))
                    n = PREPS - 1
                    pe.wait_ge(bias_ready, 2)
                    pe.wait_ge(prep_high, len(prep))
                    mm(ps_c[:, n % RING, 0:C], ln2b_rep[:, 0, :], nat_rf_t[:, 0, :], start=True, stop=False)
                    mm(ps_c[:, n % RING, 0:C], ln2b_rep[:, 1, :], nat_rf_t[:, 1, :], start=False, stop=True)\
                        .then_inc(prep_filled, 1)
                    pe.wait_ge(prep_low, splits(len(prep)) + 1)
                    pe.wait_ge(out_w_in, 16)
                    continue
                if has(prj):
                    transposes("qkv", prj, 0)
                if has(mix):
                    attention_out(mix, 0)
                if has(prj):
                    transposes("qkv", prj, 1)
                if has(mix):
                    attention_out(mix, 1)
                if has(prj):
                    project("qkv", prj, 0, qkv_w, QKV)
                if has(mix):
                    transposes("mix", mix, 0)
                if has(prj):
                    project("qkv", prj, 1, qkv_w, QKV)
                if has(mix):
                    transposes("mix", mix, 1)
                    for q in range(2):
                        project("mix", mix, q, kf_w, NH)
                        gate_rows(mix, q)
                    channel_out(mix, 0)
                    channel_out(mix, 1)
                    transposes("ffn", mix, 0)
                    project("ffn", mix, 0, in_w, NH)
                    transposes("ffn", mix, 1)
                    ffn_out(mix, 0)
                    project("ffn", mix, 1, in_w, NH)
                    ffn_out(mix, 1)


_INS = ["x", "L0_tok_weight", "L0_attn_ln1_w", "L0_attn_ln1_b", "L0_attn_ln2_w", "L0_attn_ln2_b",
        "L0_attn_decay", "L0_attn_first", "L0_attn_Wk_a", "L0_attn_Wv_a", "L0_attn_Wr_a", "L0_attn_Wo_a",
        "L0_attn_Wk_f", "L0_attn_Wv_f", "L0_attn_Wr_f", "L0_ffn_in_weight", "L0_ffn_in_bias",
        "L0_ffn_out_weight"]


def kernel(**inputs):
    import numpy as _np
    import concourse.bacc as _bacc
    from concourse import mybir as _mybir
    from concourse.bass_utils import run_bass_kernel_spmd as _run

    nc = _bacc.Bacc("TRN2", target_bir_lowering=False, num_devices=1)
    arrays, args = {}, []
    for name in _INS:
        a = _np.ascontiguousarray(inputs[name])
        arrays[f"in_{name}"] = a
        args.append(nc.dram_tensor(f"in_{name}", a.shape, _mybir.dt.from_np(a.dtype), kind="ExternalInput").ap())
    shape = tuple(inputs["x"].shape) + (inputs["L0_tok_weight"].shape[1],)
    out = nc.dram_tensor("out", shape, _mybir.dt.float32, kind="ExternalOutput").ap()
    tower(nc, *args, out)
    r = _run(nc, [arrays], core_ids=[0])
    return r.results[0]["out"]
```

```python
from contextlib import ExitStack

import concourse.bass as bass
from concourse import mybir

F32 = mybir.dt.float32
F32R = mybir.dt.float32r
I32 = mybir.dt.int32
U32 = mybir.dt.uint32
ALU = mybir.AluOpType
ACT = mybir.ActivationFunctionType

P = 128
EPS = 1e-5
M_START = -1e38


def tower(nc, x, table, ln1_w, ln1_b, ln2_w, ln2_b, decay, first, Wk, Wv, Wr, Wo, Wkf, Wvf, Wrf,
          w_in, b_in, w_out, out):
    B, T = x.shape
    VOCAB, C = table.shape
    HID = Wkf.shape[0]
    NT = T // P
    NH = HID // P
    CB = C - P
    PAIRS = B // 2
    assert T == 512 and P < C <= P + 64 and CB == 64 and HID % P == 0 and B % 2 == 0
    QKV = 5
    H0_SLOTS = 3

    steps = range(-2, PAIRS + 1)

    def has(p):
        return 0 <= p < PAIRS

    CHUNKS = {"qkv": QKV, "mix": NH + 2, "ffn": NH}
    norms = []
    for s in steps:
        for kind, p in (("qkv", s + 1), ("mix", s - 1), ("ffn", s - 1)):
            if has(p):
                norms += [(kind, p, 0), (kind, p, 1)]
    norm_no = {key: n for n, key in enumerate(norms)}
    chunks_to, n = [], 0
    for kind, _, _ in norms:
        n += CHUNKS[kind]
        chunks_to.append(n)

    def chunk_end(kind, p, q):
        return chunks_to[norm_no[kind, p, q]]

    def chunk_start(kind, p, q):
        return chunk_end(kind, p, q) - CHUNKS[kind]

    token_outs = [("attn", 0, 0)]
    for p in range(PAIRS):
        token_outs += [("attn", p, 1), ("chan", p, 0), ("chan", p, 1), ("ffn", p, 0)]
        if has(p + 1):
            token_outs.append(("attn", p + 1, 0))
        token_outs.append(("ffn", p, 1))
    out_no = {key: 2 * n for n, key in enumerate(token_outs)}

    def tile_no(p, j):
        return 3 * p + (j + 1) % 3

    with ExitStack() as ctx:
        def sb(name, shape, dt=F32):
            return ctx.enter_context(nc.sbuf_tensor(name, shape, dt))

        def sem(name):
            return ctx.enter_context(nc.semaphore(name))

        ident = sb("ident", [P, P])
        vec_rows = sb("vec_rows", [5 + NH, C])
        vec_cols = sb("vec_cols", [P, 2, 5])
        b_in_col = sb("b_in_col", [P, NH])
        wu = sb("wu", [P, 2, 2])
        bias_qkv = sb("bias_qkv", [P, QKV])
        bias_half = sb("bias_half", [P, QKV])
        bias_kf = sb("bias_kf", [P, NH])
        minus_half = sb("minus_half", [P, 2 * NT])
        qkv_w = sb("qkv_w", [P, 4, QKV * P], F32R)
        kf_w = sb("kf_w", [P, 4, HID], F32R)
        in_w = sb("in_w", [P, 4, HID], F32R)
        rf_w = sb("rf_w", [P, 4, C], F32R)
        rf_bias = sb("rf_bias", [P, C], F32R)
        rf_pick = sb("rf_pick", [P, P], F32R)
        wo_a = sb("wo_a", [P, C])
        wo_b = sb("wo_b", [P, 2, C])
        vf_w = sb("vf_w", [P, NH, C])
        out_w = sb("out_w", [P, NH, C])
        ids = sb("ids", [P, B, NT], I32)
        id_f = sb("id_f", [P, B, NT])
        id_ok = sb("id_ok", [P, B, NT])
        rows = sb("rows", [P, B * NT], U32)

        h0 = sb("h0", [P, H0_SLOTS, 2, NT, C])
        resid = sb("resid", [P, 2, NT, C])
        gate = sb("gate", [P, 2, NT, C])
        normed = sb("normed", [P, 2, NT, C])
        NE = len(norms)
        stats = sb("stats", [P, 2, NT, 6])
        mean_var = sb("mean_var", [P, NE, NT, 2])
        var_arg = sb("var_arg", [P, NE, 2, NT])
        rstd = sb("rstd", [P, NE, 2, NT])
        shift = sb("shift", [P, NE, 2, NT])

        act_a = sb("act_a", [P, 2, 2, T], F32R)
        act_b = sb("act_b", [P, 2, T], F32R)
        key = sb("key", [P, 2, 3, T])
        val = sb("val", [P, 2, 3, T])
        rec = sb("rec", [P, 2, 3, T])
        mixed = sb("mixed", [P, 3, T])
        mx = sb("mx", [P, 2 * (T + 1)])
        ex = sb("ex", [P, 4, T])
        ev = sb("ev", [P, 2, T])
        st = sb("st", [P, 4, T])
        wt = sb("wt", [P, 2, 2, T])
        cen = sb("cen", [P, 2, T])
        hid = sb("hid", [P, 2, NH, T])

        spare = hid[:].rearrange("p q m t -> p (q m t)")
        taken = [0]

        def stage(m, c):
            at = taken[0]
            taken[0] += m * c
            return spare[:, at:at + m * c].rearrange("p (m c) -> p m c", c=c)

        nat_qkv = stage(QKV, C)
        nat_wo = stage(2, C)
        nat_rf = stage(2, C)
        nat_rf_t = stage(2, C)
        ln2b_rep = stage(2, P)
        nat_kf = stage(NH, C)
        nat_in = stage(NH, C)
        ln1b_all = stage(1, C)[:, 0]
        ln2b_all = stage(1, C)[:, 0]
        rf_bias_h = stage(1, C)[:, 0]
        junk = stage(1, C)[:, 0]
        assert taken[0] <= 2 * NH * T
        nat_vf = gate[:].rearrange("p q j c -> p (q j c)").rearrange("p (m c) -> p m c", c=HID)

        ps_t = ctx.enter_context(nc.psum_tensor("ps_t", [P, 2, T], F32))
        ps_c = ctx.enter_context(nc.psum_tensor("ps_c", [P, 4, T], F32))
        ps_o = ctx.enter_context(nc.psum_tensor("ps_o", [P, 2, 512], F32))
        RING = 4

        ids_in = sem("ids_in")
        vecs_in = sem("vecs_in")
        lnb_in = sem("lnb_in")
        nat_qkv_in = sem("nat_qkv_in")
        nat_wo_in = sem("nat_wo_in")
        nat_rf_in = sem("nat_rf_in")
        nat_kf_in = sem("nat_kf_in")
        nat_in_in = sem("nat_in_in")
        nat_vf_in = sem("nat_vf_in")
        out_w_in = sem("out_w_in")
        gathered = [sem(f"gathered{b}") for b in range(B)]
        out_stored = [sem(f"out_stored{q}") for q in range(2)]
        consts = sem("consts")
        h0_cleared = sem("h0_cleared")
        rows_ready = sem("rows_ready")
        edges_ready = sem("edges_ready")
        prep_filled = sem("prep_filled")
        prep_high = sem("prep_high")
        prep_low = sem("prep_low")
        cols_ready = sem("cols_ready")
        bias_ready = sem("bias_ready")
        var_ready = sem("var_ready")
        rstd_ready = sem("rstd_ready")
        shift_ready = sem("shift_ready")
        normed_ready = sem("normed_ready")
        x0_ready = sem("x0_ready")
        res_ready = sem("res_ready")
        h1_ready = sem("h1_ready")
        t_filled = sem("t_filled")
        high_ready = sem("high_ready")
        low_ready = sem("low_ready")
        c_filled = sem("c_filled")
        c_freed = sem("c_freed")
        even_ready = sem("even_ready")
        odd_ready = sem("odd_ready")
        o_filled = sem("o_filled")
        o_freed = sem("o_freed")
        d_ready = sem("d_ready")
        e_ready = sem("e_ready")
        ev_ready = sem("ev_ready")
        w_arg = sem("w_arg")
        w_ready = sem("w_ready")
        ecv_ready = sem("ecv_ready")
        st_ready = sem("st_ready")
        sw_ready = sem("sw_ready")
        sum_ready = sem("sum_ready")
        rden_ready = sem("rden_ready")
        z_ready = sem("z_ready")
        act_step = sem("act_step")
        dve_step = sem("dve_step")
        pool_step = sem("pool_step")
        pe_step = sem("pe_step")

        prep = []
        for m in range(0, QKV, 2):
            prep.append(("split", qkv_w, nat_qkv, m, [P] * min(2, QKV - m), 0))
        prep.append(("wo", None, nat_wo, 0, [P, CB], None))
        prep.append(("rf", rf_w, nat_rf, 0, [P, CB], 1))
        for m in range(0, NH, 2):
            prep.append(("split", kf_w, nat_kf, m, [P, P], 1))
        for m in range(0, NH, 2):
            prep.append(("vf", None, nat_vf, m, [P, P], None))
        for m in range(0, NH, 2):
            prep.append(("split", in_w, nat_in, m, [P, P], None))
        SPLIT_W = {id(qkv_w): nat_qkv_in, id(kf_w): nat_kf_in, id(in_w): nat_in_in}
        PREPS = len(prep) + 2

        def prep_bank(n):
            return ps_c[:, n + 1] if n < 3 else ps_o[:, (n - 3) % 2]

        def splits(k):
            return sum(item[0] in ("split", "rf") for item in prep[:k])

        PREP_SLOTS = {-1: ((5, 7), (7, 9)), 0: ((9, 11), (11, len(prep)))}

        block = ctx.enter_context(nc.Block())

        @block.sync
        def _(sp):
            sp.dma_start(ids[:], x.rearrange("b (p j) -> p b j", j=NT)).then_inc(ids_in, 16)
            for n, v in enumerate((ln1_w, ln2_w, decay, first, ln2_b)):
                sp.dma_start(vec_rows[n:n + 1, :], v.rearrange("(a c) -> a c", a=1)).then_inc(vecs_in, 16)
            sp.dma_start(vec_rows[5:5 + NH, 0:P], b_in.rearrange("(a c) -> a c", c=P)).then_inc(vecs_in, 16)
            for m, w in enumerate((Wk, Wv, Wr)):
                sp.dma_start(nat_qkv[:, m, :], w[0:P, :]).then_inc(nat_qkv_in, 16)
            for m, half, w in ((3, 0, Wk), (3, 1, Wv), (4, 0, Wr), (4, 1, Wr)):
                sp.dma_start(nat_qkv[64 * half:64 * half + 64, m, :], w[P:C, :]).then_inc(nat_qkv_in, 16)
            sp.dma_start(ln1b_all, ln1_b.partition_broadcast(P)).then_inc(lnb_in, 16)
            sp.dma_start(ln2b_all, ln2_b.partition_broadcast(P)).then_inc(lnb_in, 16)
            for w, nat, s in ((Wo, nat_wo, nat_wo_in), (Wrf, nat_rf, nat_rf_in)):
                sp.dma_start(nat[:, 0, :], w[0:P, :]).then_inc(s, 16)
                sp.dma_start(nat[0:CB, 1, :], w[P:C, :]).then_inc(s, 16)
            sp.dma_start(nat_kf, Wkf.rearrange("(m p) c -> p m c", p=P)).then_inc(nat_kf_in, 16)
            sp.dma_start(nat_vf[:, 0, :], Wvf[0:P, :]).then_inc(nat_vf_in, 16)
            sp.dma_start(nat_vf[0:CB, 1, :], Wvf[P:C, :]).then_inc(nat_vf_in, 16)
            sp.dma_start(nat_in, w_in.rearrange("(m p) c -> p m c", p=P)).then_inc(nat_in_in, 16)
            sp.dma_start(out_w[:], w_out.rearrange("(m p) c -> p m c", p=P)).then_inc(out_w_in, 16)
            for p in range(PAIRS):
                for q in range(2):
                    sp.wait_ge(o_freed, out_no["ffn", p, q] + 2)
                    sp.dma_start(out[2 * p + q].rearrange("(p j) c -> p (j c)", j=NT),
                                 resid[:, q].rearrange("p j c -> p (j c)")).then_inc(out_stored[q], 16)
            for q in range(2):
                sp.wait_ge(out_stored[q], 16 * PAIRS)

        @block.gpsimd
        def _(pool):
            g = nc.gpsimd
            g.memset(ident[:], 0.0).then_inc(pool_step, 1)
            pool.wait_ge(pool_step, 1)
            g.affine_select(out=ident[:], in_=ident[:], compare_op=ALU.not_equal, fill=1.0, base=0,
                            pattern=[[-1, P]], channel_multiplier=1).then_inc(consts, 1)
            g.memset(minus_half[:], -0.5).then_inc(consts, 1)

            def clear_rows(p):
                if p >= H0_SLOTS:
                    pool.wait_ge(res_ready, 2 * (p - H0_SLOTS) + 2)
                g.memset(h0[:, p % H0_SLOTS], 0.0).then_inc(h0_cleared, 1)

            def gather(p, q):
                b = 2 * p + q
                pool.wait_ge(h0_cleared, p + 1)
                if b == 0:
                    pool.wait_ge(rows_ready, 1)
                for j in range(NT):
                    g.indirect_dma_start(
                        out=h0[:, p % H0_SLOTS, q, j, :], out_offset=None, in_=table,
                        in_offset=bass.IndirectOffsetOnAxis(ap=rows[:, b * NT + j:b * NT + j + 1], axis=0),
                        bounds_check=VOCAB - 1, oob_is_err=False).then_inc(gathered[b], 16)

            def inv_sqrt(kind, p, q):
                e = norm_no[kind, p, q]
                k = 2 if kind == "qkv" else 1
                if e == 0:
                    pool.wait_ge(consts, 2)
                pool.wait_ge(var_ready, e + 1)
                g.tensor_tensor(rstd[:, e, 0:k, :].rearrange("p k j -> p (k j)"),
                                var_arg[:, e, 0:k, :].rearrange("p k j -> p (k j)"),
                                minus_half[:, 0:k * NT], ALU.pow).then_inc(rstd_ready, 1)

            def first_residual(p, q):
                e = norm_no["qkv", p, q]
                pool.wait_ge(shift_ready, e + 1)
                if p:
                    pool.wait_ge(out_stored[q], 16 * p)
                for j in range(NT):
                    ins = g.tensor_scalar(resid[:, q, j, :], h0[:, p % H0_SLOTS, q, j, :],
                                          rstd[:, e, 0, j:j + 1], shift[:, e, 0, j:j + 1], ALU.mult, ALU.add)
                ins.then_inc(x0_ready, 1)

            def second_residual(p, q):
                pool.wait_ge(normed_ready, norm_no["mix", p, q] + 1)
                r = resid[:, q].rearrange("p j c -> p (j c)")
                g.tensor_tensor(r, r, h0[:, p % H0_SLOTS, q].rearrange("p j c -> p (j c)"),
                                ALU.add).then_inc(res_ready, 1)

            def weigh_values(p, j):
                t = tile_no(p, j)
                pool.wait_ge(e_ready, 2 * t + 2)
                if t:
                    pool.wait_ge(st_ready, 4 * t)
                v = val[:, p % 2, j, :].unsqueeze(1).to_broadcast([P, 2, T])
                g.tensor_tensor(ev[:], ex[:, 2:4, :], v, ALU.mult).then_inc(ev_ready, 1)

            def weigh_centre(p, j):
                t = tile_no(p, j)
                pool.wait_ge(w_ready, 2 * t + 2)
                g.tensor_tensor(cen[:, 0, :], cen[:, 1, :], val[:, p % 2, j, :],
                                ALU.mult).then_inc(ecv_ready, 1)

            def weigh_states(p, j, *parts):
                t = tile_no(p, j)
                for n in parts or (0, 1):
                    pool.wait_ge(st_ready, 4 * t + 2 * n + 2)
                    s = st[:, 2 * n:2 * n + 2, :]
                    g.tensor_tensor(s, s, wt[:, t % 2], ALU.mult).then_inc(sw_ready, 1)

            def square(p, q):
                n = chunk_start("mix", p, q)
                for m in range(0, NH, 2):
                    pool.wait_ge(c_freed, n + m + 1)
                    h = hid[:, q, m, :]
                    g.tensor_tensor(h, h, h, ALU.mult).then_inc(even_ready, 1)

            clear_rows(0)
            gather(0, 0)
            gather(0, 1)
            inv_sqrt("qkv", 0, 0)
            inv_sqrt("qkv", 0, 1)
            for s in steps[1:]:
                mix, wkv, nxt = s - 1, s, s + 2
                if has(nxt) and nxt < H0_SLOTS:
                    clear_rows(nxt)
                    gather(nxt, 0)
                    gather(nxt, 1)
                if has(mix):
                    first_residual(mix, 1)
                    second_residual(mix, 0)
                if has(wkv):
                    weigh_values(wkv, 2)
                if has(mix):
                    inv_sqrt("mix", mix, 1)
                if has(wkv):
                    weigh_centre(wkv, 2)
                    weigh_states(wkv, 2)
                if has(mix):
                    second_residual(mix, 1)
                if has(wkv):
                    weigh_values(wkv, 0)
                if has(mix):
                    square(mix, 0)
                if has(wkv):
                    weigh_centre(wkv, 0)
                    weigh_states(wkv, 0)
                if has(mix):
                    square(mix, 1)
                if has(wkv):
                    weigh_values(wkv, 1)
                if has(nxt) and nxt >= H0_SLOTS:
                    clear_rows(nxt)
                if has(mix):
                    inv_sqrt("ffn", mix, 0)
                if has(wkv):
                    weigh_centre(wkv, 1)
                    weigh_states(wkv, 1)
                if has(nxt) and nxt >= H0_SLOTS:
                    gather(nxt, 0)
                if has(mix):
                    inv_sqrt("ffn", mix, 1)
                if has(nxt):
                    if nxt >= H0_SLOTS:
                        gather(nxt, 1)
                    inv_sqrt("qkv", nxt, 0)
                    inv_sqrt("qkv", nxt, 1)
                if has(wkv):
                    first_residual(wkv, 0)
                    inv_sqrt("mix", wkv, 0)

        @block.scalar
        def _(act):
            a = nc.scalar
            own = [0]

            def after(ins):
                own[0] += 1
                ins.then_inc(act_step, 1)
                act.wait_ge(act_step, own[0])

            def prepare(first_item, last_item):
                for n, (kind, dst, nat, m, sizes, ln) in list(enumerate(prep))[first_item:last_item]:
                    bank = prep_bank(n)
                    if n == 0:
                        act.wait_ge(cols_ready, 5)
                    act.wait_ge(prep_filled, n + 2)
                    cols = sum(sizes)
                    if kind == "split" or kind == "rf":
                        if kind == "rf":
                            a.activation(nat_rf_t[:, 0, :], bank[:, 0:C], ACT.Identity).then_inc(act_step, 1)
                            a.activation(nat_rf_t[:, 1, :], bank[:, 256:256 + C], ACT.Identity).then_inc(act_step, 1)
                            own[0] += 2
                        at = m * P
                        sa = 1.0 if ln is None else vec_cols[:, 0, ln:ln + 1]
                        sb_ = 1.0 if ln is None else vec_cols[64:128, 1, ln:ln + 1]
                        a.activation(dst[:, 0, at:at + cols], bank[:, 0:cols], ACT.Identity, scale=sa)\
                            .then_inc(act_step, 1)
                        a.activation(dst[64:128, 2, at:at + cols], bank[64:128, 256:256 + cols],
                                     ACT.Identity, scale=sb_).then_inc(act_step, 1)
                        own[0] += 2
                        a.activation(dst[0:64, 2, at:at + cols], bank[64:128, 256:256 + cols],
                                     ACT.Identity, scale=sb_).then_inc(prep_high, 1)
                    elif kind == "wo":
                        a.activation(wo_a[:], bank[:, 0:C], ACT.Identity, scale=0.5).then_inc(act_step, 1)
                        own[0] += 1
                        act.wait_ge(edges_ready, 3)
                        a.activation(wo_b[0:64, 0, :], bank[64:128, 256:256 + C], ACT.Identity, scale=0.5)\
                            .then_inc(act_step, 1)
                        own[0] += 1
                        a.activation(wo_b[64:128, 1, :], bank[64:128, 256:256 + C], ACT.Identity, scale=0.5)\
                            .then_inc(prep_high, 1)
                    else:
                        a.activation(vf_w[:, m:m + 2, :], bank[:, 0:2 * C].rearrange("p (m c) -> p m c", c=C),
                                     ACT.Identity, scale=0.5).then_inc(prep_high, 1)

            def round_high(kind, p, q):
                e = norm_no[kind, p, q]
                act.wait_ge(t_filled, e + 1)
                if e >= 2:
                    act.wait_ge(c_filled, chunks_to[e - 2])
                a.activation(act_a[:, e % 2, 0, :], ps_t[:, 0], ACT.Identity).then_inc(high_ready, 1)
                a.activation(act_b[64:128, e % 2, :], ps_t[64:128, 1], ACT.Identity).then_inc(high_ready, 1)

            def take_qkv(p, q):
                n, slot = chunk_start("qkv", p, q), p % 2
                if p >= 2:
                    act.wait_ge(z_ready, tile_no(p - 2, q) + 1)
                bank = [ps_c[:, (n + i) % RING] for i in range(QKV)]
                act.wait_ge(c_filled, n + 1)
                if n == 0:
                    act.wait_ge(bias_ready, 1)
                a.activation(key[:, slot, q, :], bank[0], ACT.Identity, bias=bias_qkv[:, 0:1]).then_inc(c_freed, 1)
                act.wait_ge(c_filled, n + 2)
                a.activation(val[:, slot, q, :], bank[1], ACT.Identity, bias=bias_qkv[:, 1:2]).then_inc(c_freed, 1)
                act.wait_ge(c_filled, n + 3)
                a.activation(rec[:, slot, q, :], bank[2], ACT.Tanh, bias=bias_half[:, 2:3], scale=0.5)\
                    .then_inc(c_freed, 1)
                act.wait_ge(c_filled, n + 4)
                mine = slice(64 * q, 64 * q + 64)
                own[0] += 1
                a.activation(key[mine, slot, 2, :], bank[3][0:64], ACT.Identity, bias=bias_qkv[0:64, 3:4])\
                    .then_inc(act_step, 1)
                a.activation(val[mine, slot, 2, :], bank[3][64:128], ACT.Identity, bias=bias_qkv[64:128, 3:4])\
                    .then_inc(c_freed, 1)
                act.wait_ge(c_filled, n + 5)
                a.activation(rec[mine, slot, 2, :], bank[4][mine], ACT.Tanh, bias=bias_half[mine, 4:5], scale=0.5)\
                    .then_inc(c_freed, 1)

            def exp_steps(p, j):
                t, part = tile_no(p, j), j // 2
                act.wait_ge(d_ready, 2 * t + 1)
                a.activation(ex[:, 0:2, :], ex[:, 0:2, :], ACT.Exp, bias=wu[:, part, 0:1]).then_inc(e_ready, 1)
                act.wait_ge(d_ready, 2 * t + 2)
                a.activation(ex[:, 2:4, :], ex[:, 2:4, :], ACT.Exp).then_inc(e_ready, 1)

            def exp_weights(p, j):
                t, part = tile_no(p, j), j // 2
                act.wait_ge(w_arg, 2 * t + 1)
                a.activation(wt[:, t % 2], wt[:, t % 2], ACT.Exp).then_inc(w_ready, 1)
                act.wait_ge(w_arg, 2 * t + 2)
                a.activation(cen[:, 1, :], cen[:, 1, :], ACT.Exp, bias=wu[:, part, 1:2])\
                    .then_inc(w_ready, 1)

            def invert(p, j):
                t = tile_no(p, j)
                act.wait_ge(sum_ready, t + 1)
                d = wt[:, t % 2, 1, :]
                after(a.activation(d, d, ACT.Ln))
                a.activation(d, d, ACT.Exp, scale=-1.0).then_inc(rden_ready, 1)

            def take_mix(p, q):
                n = chunk_start("mix", p, q)
                if p:
                    act.wait_ge(o_filled, out_no["ffn", p - 1, q] + 2)
                for m in range(NH):
                    act.wait_ge(c_filled, n + m + 1)
                    a.activation(hid[:, q, m, :], ps_c[:, (n + m) % RING], ACT.Relu, bias=bias_kf[:, m:m + 1])\
                        .then_inc(c_freed, 1)

            def take_gate(p, q, h):
                n = chunk_start("mix", p, q)
                if p and h == 0:
                    act.wait_ge(h1_ready, 2 * p + q - 1)
                act.wait_ge(c_filled, n + NH + h + 1)
                a.activation(gate[:, q, 2 * h:2 * h + 2, :].rearrange("p j c -> p (j c)"),
                             ps_c[:, (n + NH + h) % RING, 0:2 * C], ACT.Tanh, scale=0.5).then_inc(c_freed, 1)

            def take_ffn(p, q):
                n = chunk_start("ffn", p, q)
                act.wait_ge(o_filled, out_no["chan", p, q] + 2)
                for m in range(NH):
                    act.wait_ge(c_filled, n + m + 1)
                    a.activation(hid[:, q, m, :], ps_c[:, (n + m) % RING], ACT.Gelu, bias=b_in_col[:, m:m + 1])\
                        .then_inc(c_freed, 1)

            prepare(0, 5)
            round_high("qkv", 0, 0)
            for s in steps[1:]:
                mix, wkv, prj, nxt = s - 1, s, s + 1, s + 2
                if has(prj):
                    round_high("qkv", prj, 1)
                    take_qkv(prj, 0)
                if s in PREP_SLOTS:
                    prepare(*PREP_SLOTS[s][0])
                if has(wkv):
                    exp_steps(wkv, 2)
                if has(mix):
                    round_high("mix", mix, 0)
                if has(prj):
                    take_qkv(prj, 1)
                if has(wkv):
                    exp_weights(wkv, 2)
                if s in PREP_SLOTS:
                    prepare(*PREP_SLOTS[s][1])
                if s == 0:
                    act.wait_ge(prep_filled, PREPS)
                    bank = prep_bank(len(prep))
                    a.activation(rf_bias[0:1, :], bank[0:1, 0:C], ACT.Identity).then_inc(act_step, 1)
                    own[0] += 1
                    a.activation(rf_bias_h[32:33, :].bitcast(F32R), bank[32:33, 0:C], ACT.Identity)\
                        .then_inc(prep_high, 1)
                if has(mix) and has(prj):
                    round_high("mix", mix, 1)
                if has(mix):
                    take_mix(mix, 0)
                if has(wkv):
                    exp_steps(wkv, 0)
                if has(mix):
                    take_gate(mix, 0, 0)
                    take_gate(mix, 0, 1)
                if has(mix) and not has(prj):
                    round_high("mix", mix, 1)
                if has(wkv):
                    invert(wkv, 2)
                    exp_weights(wkv, 0)
                if has(mix):
                    take_mix(mix, 1)
                if has(wkv):
                    exp_steps(wkv, 1)
                if has(mix):
                    take_gate(mix, 1, 0)
                    take_gate(mix, 1, 1)
                if has(wkv):
                    invert(wkv, 0)
                    exp_weights(wkv, 1)
                if has(mix):
                    round_high("ffn", mix, 0)
                    take_ffn(mix, 0)
                if has(wkv):
                    invert(wkv, 1)
                if has(mix):
                    round_high("ffn", mix, 1)
                    take_ffn(mix, 1)
                if has(nxt):
                    round_high("qkv", nxt, 0)

        @block.vector
        def _(dve):
            v = nc.vector
            own = [0]

            def step(ins):
                own[0] += 1
                ins.then_inc(dve_step, 1)
                return own[0]

            def after(ins):
                dve.wait_ge(dve_step, step(ins))

            def set_up():
                dve.wait_ge(ids_in, 16)
                after(v.tensor_scalar(id_ok[:], ids[:], 0.0, None, ALU.is_ge))
                after(v.scalar_tensor_tensor(id_ok[:], ids[:], float(VOCAB), id_ok[:], ALU.is_lt, ALU.mult))
                after(v.scalar_tensor_tensor(id_f[:], ids[:], -float(VOCAB), id_ok[:], ALU.add, ALU.mult))
                v.tensor_scalar(rows[:], id_f[:].rearrange("p b j -> p (b j)"), float(VOCAB), None, ALU.add)\
                    .then_inc(rows_ready, 1)
                dve.wait_ge(prep_filled, 1)
                bank = ps_c[:, 0]
                v.tensor_copy(vec_cols[:, 0, :], bank[:, 0:5]).then_inc(cols_ready, 1)
                v.tensor_copy(vec_cols[64:128, 1, :], bank[64:128, 16:21]).then_inc(cols_ready, 1)
                v.tensor_copy(vec_cols[0:64, 1, :], bank[64:128, 16:21]).then_inc(cols_ready, 1)
                v.tensor_copy(b_in_col[:], bank[:, 5:5 + NH]).then_inc(cols_ready, 1)
                dve.wait_ge(cols_ready, 4)
                v.tensor_scalar(wu[:], vec_cols[:, :, 2:4], 1.0 / T, None, ALU.mult).then_inc(cols_ready, 1)

            def set_edges():
                step(v.memset(mx[:, 0:1], M_START))
                step(v.memset(mx[:, 2 * T + 1:2 * T + 2], M_START))
                for n, edge in ((0, 0), (1, T - 1), (2, 0), (3, T - 1)):
                    step(v.memset(st[:, n, edge:edge + 1], 0.0))
                v.memset(wo_b[:], 0.0).then_inc(edges_ready, 1)
                v.memset(rf_bias[:].bitcast(F32), 0.0).then_inc(edges_ready, 1)
                v.memset(rf_pick[:].bitcast(F32), 0.0).then_inc(edges_ready, 1)
                dve.wait_ge(edges_ready, 3)
                step(v.memset(rf_pick[0:1, :].bitcast(F32), 1.0))
                step(v.memset(rf_pick[32:33, :].bitcast(F32), 1.0))

            def fold_bias(bias, w, lnb, m):
                after(v.scalar_tensor_tensor(junk, w[:, m, :], 1.0, lnb, ALU.mult, ALU.mult,
                                             accum_out=bias[:, m:m + 1]))

            def prepare(first_item, last_item):
                for n, (kind, dst, nat, m, sizes, ln) in list(enumerate(prep))[first_item:last_item]:
                    bank = prep_bank(n)
                    if kind not in ("split", "rf"):
                        continue
                    dve.wait_ge(prep_high, n + 1)
                    cols, at = sum(sizes), m * P
                    sa = 1.0 if ln is None else vec_cols[:, 0, ln:ln + 1]
                    sb_ = 1.0 if ln is None else vec_cols[64:128, 1, ln:ln + 1]
                    step(v.scalar_tensor_tensor(dst[:, 1, at:at + cols], bank[:, 0:cols], sa,
                                                dst[:, 0, at:at + cols].bitcast(F32), ALU.mult, ALU.subtract))
                    for half in (1, 0):
                        ins = v.scalar_tensor_tensor(dst[64 * half:64 * half + 64, 3, at:at + cols],
                                                     bank[64:128, 256:256 + cols], sb_,
                                                     dst[64:128, 2, at:at + cols].bitcast(F32),
                                                     ALU.mult, ALU.subtract)
                        if half:
                            step(ins)
                    ins.then_inc(prep_low, 1)

            def statistics(kind, p, q, src):
                e = norm_no[kind, p, q]
                for j in range(NT):
                    done = step(v.bn_stats(stats[:, e % 2, j, :], src[:, j, :]))
                for j in range(NT):
                    dve.wait_ge(dve_step, done - NT + 1 + j)
                    last = step(v.bn_aggr(mean_var[:, e, j, :], stats[:, e % 2, j, :]))
                dve.wait_ge(dve_step, last)
                var = mean_var[:, e, :, 1]
                if kind == "qkv":
                    step(v.tensor_scalar(var_arg[:, e, 1, :], var, 1.0 + EPS, EPS * EPS, ALU.mult, ALU.add))
                v.tensor_scalar(var_arg[:, e, 0, :], var, EPS, None, ALU.add).then_inc(var_ready, 1)

            def normalise(kind, p, q, src):
                e = norm_no[kind, p, q]
                k = 2 if kind == "qkv" else 1
                dve.wait_ge(rstd_ready, e + 1)
                mean = mean_var[:, e, :, 0].unsqueeze(1).to_broadcast([P, k, NT])
                v.scalar_tensor_tensor(shift[:, e, 0:k, :], mean, -1.0, rstd[:, e, 0:k, :],
                                       ALU.mult, ALU.mult).then_inc(shift_ready, 1)
                dve.wait_ge(shift_ready, e + 1)
                if e >= 2:
                    dve.wait_ge(t_filled, e - 1)
                for j in range(NT):
                    ins = v.tensor_scalar(normed[:, e % 2, j, :], src[:, j, :], rstd[:, e, k - 1, j:j + 1],
                                          shift[:, e, k - 1, j:j + 1], ALU.mult, ALU.add)
                    if j < NT - 1:
                        step(ins)
                ins.then_inc(normed_ready, 1)

            def embed_statistics(p, q):
                dve.wait_ge(gathered[2 * p + q], 16 * NT)
                statistics("qkv", p, q, h0[:, p % H0_SLOTS, q])

            def embed_normalise(p, q):
                normalise("qkv", p, q, h0[:, p % H0_SLOTS, q])

            def split_low(kind, p, q):
                e = norm_no[kind, p, q]
                dve.wait_ge(high_ready, 2 * e + 1)
                v.tensor_tensor(act_a[:, e % 2, 1, :], ps_t[:, 0], act_a[:, e % 2, 0, :].bitcast(F32),
                                ALU.subtract).then_inc(low_ready, 1)
                dve.wait_ge(high_ready, 2 * e + 2)
                v.tensor_tensor(act_b[0:64, e % 2, :], ps_t[64:128, 1], act_b[64:128, e % 2, :].bitcast(F32),
                                ALU.subtract).then_inc(low_ready, 1)

            mx_excl = bass.AP(mx, 0, [[2 * (T + 1), P], [T + 2, 2], [1, T]])
            mx_incl = bass.AP(mx, 1, [[2 * (T + 1), P], [T, 2], [1, T]])
            mx_b = mx[:, T + 1:2 * T + 2]

            def maxima(p, j):
                t, part, k = tile_no(p, j), j // 2, key[:, p % 2, j, :]
                w = wu[:, part, 0:1].to_broadcast([P, T])
                dve.wait_ge(c_freed, chunk_end("qkv", p, 1 if j else 0))
                if t:
                    dve.wait_ge(w_arg, 2 * t - 1)
                step(v.tensor_tensor_scan(mx[:, 1:T + 1], w, k, M_START, ALU.add, ALU.max))
                done = step(v.tensor_tensor_scan(bass.AP(mx, 2 * T, [[2 * (T + 1), P], [-1, T]]),
                                                 w, bass.AP(key, ((p % 2) * 3 + j) * T + T - 1, [[6 * T, P], [-1, T]]),
                                                 M_START, ALU.add, ALU.max))
                dve.wait_ge(dve_step, done)
                v.tensor_tensor(ex[:, 0:2, :], mx_excl, mx_incl, ALU.subtract).then_inc(d_ready, 1)
                v.tensor_tensor(ex[:, 2:4, :], k.unsqueeze(1).to_broadcast([P, 2, T]), mx_incl, ALU.subtract)\
                    .then_inc(d_ready, 1)

            def common_max(p, j):
                t, part, k = tile_no(p, j), j // 2, key[:, p % 2, j, :]
                m = cen[:, 0, :]
                if t:
                    dve.wait_ge(sum_ready, t)
                if t >= 2:
                    dve.wait_ge(z_ready, t - 1)
                after(v.tensor_tensor(m, mx[:, 0:T], mx_b[:, 1:T + 1], ALU.max))
                after(v.scalar_tensor_tensor(m, k, wu[:, part, 1:2], m, ALU.add, ALU.max))
                v.tensor_tensor(wt[:, t % 2], mx_excl, m.unsqueeze(1).to_broadcast([P, 2, T]), ALU.subtract)\
                    .then_inc(w_arg, 1)
                v.tensor_tensor(cen[:, 1, :], k, m, ALU.subtract).then_inc(w_arg, 1)

            def back(tile, offset, count):
                return bass.AP(tile[:].tensor, offset, [[tile[:].ap[0][0], P], [-1, count]])

            def scans(p, j):
                t = tile_no(p, j)
                for n, (data, base) in enumerate(((ev, 0), (ex, 2 * T))):
                    if n == 0:
                        dve.wait_ge(ev_ready, t + 1)
                    src = ev[:, 0, :] if n == 0 else ex[:, 2, :]
                    v.tensor_tensor_scan(st[:, 2 * n, 1:T], ex[:, 0, 0:T - 1], src[:, 0:T - 1], 0.0,
                                         ALU.mult, ALU.add).then_inc(st_ready, 1)
                    v.tensor_tensor_scan(back(st, (2 * n + 1) * T + T - 2, T - 1),
                                         back(ex, T + T - 1, T - 1), back(data, base + T + T - 1, T - 1), 0.0,
                                         ALU.mult, ALU.add).then_inc(st_ready, 1)

            def sums(p, j):
                t = tile_no(p, j)
                dve.wait_ge(sw_ready, 2 * t + 2)
                dve.wait_ge(ecv_ready, t + 1)
                s = st[:].rearrange("p (n d) t -> p n d t", d=2)
                after(v.tensor_tensor(wt[:, t % 2], s[:, :, 0, :], s[:, :, 1, :], ALU.add))
                v.tensor_tensor(wt[:, t % 2], wt[:, t % 2], cen[:], ALU.add).then_inc(sum_ready, 1)

            def gated(p, j):
                t = tile_no(p, j)
                dve.wait_ge(rden_ready, t + 1)
                y, r = wt[:, t % 2, 0, :], rec[:, p % 2, j, :]
                after(v.tensor_tensor(y, y, wt[:, t % 2, 1, :], ALU.mult))
                if p:
                    dve.wait_ge(o_filled, out_no["attn", p - 1, min(j, 1)] + 2)
                v.scalar_tensor_tensor(mixed[:, j, :], r, 1.0, y, ALU.add, ALU.mult).then_inc(z_ready, 1)

            def add_attention(p, q):
                n = out_no["attn", p, q]
                dve.wait_ge(x0_ready, 2 * p + q + 1)
                for h in range(2):
                    dve.wait_ge(o_filled, n + h + 1)
                    r = resid[:, q, 2 * h:2 * h + 2, :].rearrange("p j c -> p (j c)")
                    v.tensor_tensor(r, ps_o[:, h, 0:2 * C], r, ALU.add).then_inc(o_freed, 1)
                dve.wait_ge(o_freed, n + 2)
                statistics("mix", p, q, resid[:, q])

            def square(p, q):
                n = chunk_start("mix", p, q)
                for m in range(1, NH, 2):
                    dve.wait_ge(c_freed, n + m + 1)
                    h = hid[:, q, m, :]
                    v.tensor_tensor(h, h, h, ALU.mult).then_inc(odd_ready, 1)

            def add_channel_mix(p, q):
                n = out_no["chan", p, q]
                dve.wait_ge(c_freed, chunk_end("mix", p, q))
                for h in range(2):
                    dve.wait_ge(o_filled, n + h + 1)
                    g = gate[:, q, 2 * h:2 * h + 2, :].rearrange("p j c -> p (j c)")
                    v.scalar_tensor_tensor(g, g, 1.0, ps_o[:, h, 0:2 * C], ALU.add, ALU.mult).then_inc(o_freed, 1)
                dve.wait_ge(o_freed, n + 2)
                dve.wait_ge(res_ready, 2 * p + q + 1)
                r = resid[:, q].rearrange("p j c -> p (j c)")
                v.tensor_tensor(r, r, gate[:, q].rearrange("p j c -> p (j c)"), ALU.add).then_inc(h1_ready, 1)
                dve.wait_ge(h1_ready, 2 * p + q + 1)
                statistics("ffn", p, q, resid[:, q])

            def add_ffn(p, q):
                n = out_no["ffn", p, q]
                for h in range(2):
                    dve.wait_ge(o_filled, n + h + 1)
                    r = resid[:, q, 2 * h:2 * h + 2, :].rearrange("p j c -> p (j c)")
                    v.tensor_tensor(r, ps_o[:, h, 0:2 * C], r, ALU.add).then_inc(o_freed, 1)

            def fold_channel_biases():
                dve.wait_ge(nat_kf_in, 16)
                for m in range(NH):
                    fold_bias(bias_kf, nat_kf, ln2b_all, m)
                step(v.tensor_copy(ln2b_rep[:, 0, :], vec_cols[:, 0, 4:5].to_broadcast([P, P])))
                step(v.memset(ln2b_rep[0:64, 1, :], 0.0))
                v.tensor_copy(ln2b_rep[64:128, 1, :], vec_cols[64:128, 1, 4:5].to_broadcast([64, P]))\
                    .then_inc(bias_ready, 1)

            set_up()
            set_edges()
            embed_statistics(0, 0)
            prepare(0, 1)
            embed_normalise(0, 0)
            prepare(1, 3)
            embed_statistics(0, 1)
            split_low("qkv", 0, 0)
            dve.wait_ge(lnb_in, 32)
            dve.wait_ge(nat_qkv_in, 16 * 7)
            for m in range(QKV):
                fold_bias(bias_qkv, nat_qkv, ln1b_all, m)
            v.tensor_scalar(bias_half[:], bias_qkv[:], 0.5, None, ALU.mult).then_inc(bias_ready, 1)
            embed_normalise(0, 1)
            for s in steps[1:]:
                mix, wkv, prj, nxt = s - 1, s, s + 1, s + 2
                if has(prj):
                    split_low("qkv", prj, 1)
                if s == -1:
                    prepare(3, 5)
                if s in PREP_SLOTS:
                    prepare(*PREP_SLOTS[s][0])
                if has(mix):
                    normalise("mix", mix, 0, resid[:, 0])
                if has(wkv):
                    maxima(wkv, 2)
                if has(mix):
                    add_attention(mix, 1)
                if has(wkv):
                    common_max(wkv, 2)
                if s in PREP_SLOTS:
                    prepare(*PREP_SLOTS[s][1])
                if s == 0:
                    dve.wait_ge(prep_high, len(prep) + 1)
                    v.tensor_tensor(rf_bias[32:33, :], prep_bank(len(prep))[32:33, 0:C],
                                    rf_bias_h[32:33, :], ALU.subtract).then_inc(prep_low, 1)
                if has(mix):
                    split_low("mix", mix, 0)
                    normalise("mix", mix, 1, resid[:, 1])
                if has(wkv):
                    scans(wkv, 2)
                    maxima(wkv, 0)
                if has(mix):
                    split_low("mix", mix, 1)
                if has(wkv):
                    sums(wkv, 2)
                    common_max(wkv, 0)
                    scans(wkv, 0)
                if has(wkv):
                    gated(wkv, 2)
                if has(mix):
                    square(mix, 0)
                if has(wkv):
                    maxima(wkv, 1)
                    sums(wkv, 0)
                    common_max(wkv, 1)
                if has(mix):
                    square(mix, 1)
                    add_channel_mix(mix, 0)
                if has(wkv):
                    scans(wkv, 1)
                if has(mix):
                    normalise("ffn", mix, 0, resid[:, 0])
                if has(wkv):
                    gated(wkv, 0)
                if has(mix):
                    split_low("ffn", mix, 0)
                    add_channel_mix(mix, 1)
                if has(wkv):
                    sums(wkv, 1)
                if has(mix):
                    normalise("ffn", mix, 1, resid[:, 1])
                if has(nxt):
                    embed_statistics(nxt, 0)
                    embed_statistics(nxt, 1)
                if has(mix):
                    split_low("ffn", mix, 1)
                if has(nxt):
                    embed_normalise(nxt, 0)
                    embed_normalise(nxt, 1)
                if s == -1:
                    fold_channel_biases()
                if has(wkv):
                    gated(wkv, 1)
                if has(mix):
                    add_ffn(mix, 0)
                if has(wkv):
                    add_attention(wkv, 0)
                if has(nxt):
                    split_low("qkv", nxt, 0)
                if has(mix):
                    add_ffn(mix, 1)

        @block.tensor
        def _(pe):
            mm = nc.tensor.matmul

            def turn(dst, src, rows_in):
                return nc.tensor.transpose(dst, src, ident[0:rows_in, 0:rows_in])

            def prepare(first_item, last_item):
                for n, (kind, dst, nat, m, sizes, ln) in list(enumerate(prep))[first_item:last_item]:
                    bank = prep_bank(n)
                    if kind == "split":
                        sem_in = SPLIT_W[id(dst)]
                        pe.wait_ge(sem_in, 16 * 7 if sem_in is nat_qkv_in else 16)
                    else:
                        pe.wait_ge({"wo": nat_wo_in, "rf": nat_rf_in, "vf": nat_vf_in}[kind], 32)
                    if n >= 5:
                        pe.wait_ge(prep_high, n - 1)
                        pe.wait_ge(prep_low, splits(n - 1))
                    at = 0
                    if kind == "vf":
                        for i in range(2):
                            c = slice((m + i) * P, (m + i + 1) * P)
                            turn(bank[:, i * C:i * C + P], nat[:, 0, c], P)
                            ins = turn(bank[:, i * C + P:i * C + C], nat[0:CB, 1, c], CB)
                    else:
                        for i, size in enumerate(sizes):
                            turn(bank[:, at:at + size], nat[0:size, m + i, 0:P], size)
                            ins = turn(bank[:, 256 + at:256 + at + size], nat[0:size, m + i, C - P:C], size)
                            at += size
                    ins.then_inc(prep_filled, 1)

            def transposes(kind, p, q):
                e = norm_no[kind, p, q]
                pe.wait_ge(normed_ready, e + 1)
                if e:
                    pe.wait_ge(low_ready, 2 * e)
                for j in range(NT):
                    cols = slice(j, T, NT) if kind == "qkv" else slice(j * P, (j + 1) * P)
                    turn(ps_t[:, 0, cols], normed[:, e % 2, j, 0:P], P)
                    ins = turn(ps_t[:, 1, cols], normed[:, e % 2, j, C - P:C], P)
                ins.then_inc(t_filled, 1)

            def project(kind, p, q, w, chunks):
                e = norm_no[kind, p, q]
                n = chunk_start(kind, p, q)
                pe.wait_ge(low_ready, 2 * e + 2)
                high, low, b = act_a[:, e % 2, 0, :], act_a[:, e % 2, 1, :], act_b[:, e % 2, :]
                for m in range(chunks):
                    if n + m >= RING:
                        pe.wait_ge(c_freed, n + m + 1 - RING)
                    o, c = ps_c[:, (n + m) % RING], slice(m * P, (m + 1) * P)
                    mm(o, w[:, 0, c], high, start=True, stop=False)
                    mm(o, w[:, 1, c], high, start=False, stop=False)
                    mm(o, w[:, 0, c], low, start=False, stop=False)
                    mm(o, w[:, 2, c], b, start=False, stop=False)
                    mm(o, w[:, 3, c], b, start=False, stop=True).then_inc(c_filled, 1)

            def gate_rows(p, q, halves=(0, 1)):
                e = norm_no["mix", p, q]
                n = chunk_start("mix", p, q) + NH
                for h in halves:
                    pe.wait_ge(c_freed, n + h + 1 - RING)
                    for i in range(2):
                        tok = slice((2 * h + i) * P, (2 * h + i + 1) * P)
                        o = ps_c[:, (n + h) % RING, i * C:(i + 1) * C]
                        high, low, b = act_a[:, e % 2, 0, tok], act_a[:, e % 2, 1, tok], act_b[:, e % 2, tok]
                        mm(o, high, rf_w[:, 0, :], start=True, stop=False)
                        mm(o, high, rf_w[:, 1, :], start=False, stop=False)
                        mm(o, low, rf_w[:, 0, :], start=False, stop=False)
                        mm(o, b, rf_w[:, 2, :], start=False, stop=False)
                        mm(o, b, rf_w[:, 3, :], start=False, stop=False)
                        ins = mm(o, rf_pick[:], rf_bias[:], start=False, stop=True)
                    ins.then_inc(c_filled, 1)

            def attention_out(p, q):
                n = out_no["attn", p, q]
                pe.wait_ge(z_ready, tile_no(p, q) + 1)
                for h in range(2):
                    if n + h >= 2:
                        pe.wait_ge(o_freed, n + h - 1)
                    for i in range(2):
                        o, tok = ps_o[:, h, i * C:(i + 1) * C], slice(2 * h + i, T, NT)
                        mm(o, mixed[:, q, tok], wo_a[:], start=True, stop=False)
                        ins = mm(o, mixed[:, 2, tok], wo_b[:, q, :], start=False, stop=True)
                    ins.then_inc(o_filled, 1)

            def hidden_out(kind, p, q, w, tiles, chunk_ready):
                n = out_no[kind, p, q]
                for j in tiles:
                    h, i = divmod(j, 2)
                    if i == 0:
                        pe.wait_ge(o_freed, n + h - 1)
                    o = ps_o[:, h, i * C:(i + 1) * C]
                    for m in range(NH):
                        if j == 0:
                            pe.wait_ge(*chunk_ready(m))
                        ins = mm(o, hid[:, q, m, j * P:(j + 1) * P], w[:, m, :],
                                 start=(m == 0), stop=(m == NH - 1))
                    if i == 1:
                        ins.then_inc(o_filled, 1)

            def channel_out(p, q, tiles=range(NT)):
                hidden_out("chan", p, q, vf_w, tiles, lambda m: (odd_ready if m % 2 else even_ready,
                                                                 (2 * p + q) * NH // 2 + m // 2 + 1))

            def ffn_out(p, q):
                hidden_out("ffn", p, q, out_w, range(NT),
                           lambda m: (c_freed, chunk_start("ffn", p, q) + m + 1))

            pe.wait_ge(consts, 1)
            pe.wait_ge(vecs_in, 16 * 6)
            turn(ps_c[:, 0, 0:5 + NH], vec_rows[:, 0:P], 5 + NH)
            turn(ps_c[:, 0, 16:21], vec_rows[0:5, C - P:C], 5).then_inc(prep_filled, 1)
            prepare(0, 5)
            transposes("qkv", 0, 0)
            for s in steps[1:]:
                mix, wkv, prj, nxt = s - 1, s, s + 1, s + 2
                if has(prj):
                    transposes("qkv", prj, 1)
                if has(prj) and has(mix):
                    attention_out(mix, 1)
                if has(prj):
                    if prj == 0:
                        pe.wait_ge(prep_low, splits(3))
                    project("qkv", prj, 0, qkv_w, QKV)
                if s in PREP_SLOTS:
                    prepare(*PREP_SLOTS[s][0])
                if has(mix):
                    transposes("mix", mix, 0)
                if has(mix) and not has(prj):
                    attention_out(mix, 1)
                if has(prj):
                    project("qkv", prj, 1, qkv_w, QKV)
                if s in PREP_SLOTS:
                    prepare(*PREP_SLOTS[s][1])
                if s == 0:
                    pe.wait_ge(bias_ready, 2)
                    pe.wait_ge(prep_high, len(prep))
                    pe.wait_ge(prep_low, splits(len(prep) - 1))
                    o = prep_bank(len(prep))[:, 0:C]
                    mm(o, ln2b_rep[:, 0, :], nat_rf_t[:, 0, :], start=True, stop=False)
                    mm(o, ln2b_rep[:, 1, :], nat_rf_t[:, 1, :], start=False, stop=True).then_inc(prep_filled, 1)
                    pe.wait_ge(prep_low, splits(len(prep)) + 1)
                    pe.wait_ge(out_w_in, 16)
                if has(mix) and has(prj):
                    transposes("mix", mix, 1)
                if has(mix):
                    project("mix", mix, 0, kf_w, NH)
                    gate_rows(mix, 0)
                if has(mix) and not has(prj):
                    transposes("mix", mix, 1)
                if has(mix):
                    project("mix", mix, 1, kf_w, NH)
                    channel_out(mix, 0)
                    gate_rows(mix, 1)
                    channel_out(mix, 1, range(NT - 1))
                    transposes("ffn", mix, 0)
                    channel_out(mix, 1, [NT - 1])
                    project("ffn", mix, 0, in_w, NH)
                    transposes("ffn", mix, 1)
                    ffn_out(mix, 0)
                    project("ffn", mix, 1, in_w, NH)
                if has(wkv):
                    attention_out(wkv, 0)
                if has(nxt):
                    transposes("qkv", nxt, 0)
                if has(mix):
                    ffn_out(mix, 1)


_INS = ["x", "L0_tok_weight", "L0_attn_ln1_w", "L0_attn_ln1_b", "L0_attn_ln2_w", "L0_attn_ln2_b",
        "L0_attn_decay", "L0_attn_first", "L0_attn_Wk_a", "L0_attn_Wv_a", "L0_attn_Wr_a", "L0_attn_Wo_a",
        "L0_attn_Wk_f", "L0_attn_Wv_f", "L0_attn_Wr_f", "L0_ffn_in_weight", "L0_ffn_in_bias",
        "L0_ffn_out_weight"]


def kernel(**inputs):
    import numpy as _np
    import concourse.bacc as _bacc
    from concourse import mybir as _mybir
    from concourse.bass_utils import run_bass_kernel_spmd as _run

    nc = _bacc.Bacc("TRN2", target_bir_lowering=False, num_devices=1)
    arrays, args = {}, []
    for name in _INS:
        a = _np.ascontiguousarray(inputs[name])
        arrays[f"in_{name}"] = a
        args.append(nc.dram_tensor(f"in_{name}", a.shape, _mybir.dt.from_np(a.dtype), kind="ExternalInput").ap())
    shape = tuple(inputs["x"].shape) + (inputs["L0_tok_weight"].shape[1],)
    out = nc.dram_tensor("out", shape, _mybir.dt.float32, kind="ExternalOutput").ap()
    tower(nc, *args, out)
    r = _run(nc, [arrays], core_ids=[0])
    return r.results[0]["out"]
```

```python
from contextlib import ExitStack

import concourse.bass as bass
from concourse import mybir

F32 = mybir.dt.float32
F32R = mybir.dt.float32r
I32 = mybir.dt.int32
U32 = mybir.dt.uint32
ALU = mybir.AluOpType
ACT = mybir.ActivationFunctionType

P = 128
EPS = 1e-5
M_START = -1e38


def tower(nc, x, table, ln1_w, ln1_b, ln2_w, ln2_b, decay, first, Wk, Wv, Wr, Wo, Wkf, Wvf, Wrf,
          w_in, b_in, w_out, out):
    B, T = x.shape
    VOCAB, C = table.shape
    HID = Wkf.shape[0]
    NT = T // P
    NH = HID // P
    CB = C - P
    PAIRS = B // 2
    assert B == 8 and HID == 6 * P
    assert T == 512 and P < C <= P + 64 and CB == 64 and HID % P == 0 and B % 2 == 0
    QKV = 5
    H0_SLOTS = 3

    steps = range(-2, PAIRS + 1)

    def has(p):
        return 0 <= p < PAIRS

    CHUNKS = {"qkv": QKV, "mix": NH + 2, "ffn": NH}
    norms = []
    for s in steps:
        for kind, p in (("qkv", s + 1), ("mix", s - 1), ("ffn", s - 1)):
            if has(p):
                norms += [(kind, p, 0), (kind, p, 1)]
    norm_no = {key: n for n, key in enumerate(norms)}
    chunks_to, n = [], 0
    for kind, _, _ in norms:
        n += CHUNKS[kind]
        chunks_to.append(n)

    def chunk_end(kind, p, q):
        return chunks_to[norm_no[kind, p, q]]

    def chunk_start(kind, p, q):
        return chunk_end(kind, p, q) - CHUNKS[kind]

    def taken_to(what, p, j):
        chunk = {"key": (1, 4), "value": (2, 4), "receptance": (3, 5)}[what][j == 2]
        return chunk_start("qkv", p, min(j, 1)) + chunk

    token_outs = [("attn", 0, 0)]
    for p in range(PAIRS):
        token_outs += [("attn", p, 1), ("chan", p, 0), ("chan", p, 1), ("ffn", p, 0)]
        if has(p + 1):
            token_outs.append(("attn", p + 1, 0))
        token_outs.append(("ffn", p, 1))
    out_no = {key: 2 * n for n, key in enumerate(token_outs)}

    def tile_no(p, j):
        return 3 * p + (0, 2, 1)[j]

    with ExitStack() as ctx:
        def sb(name, shape, dt=F32):
            return ctx.enter_context(nc.sbuf_tensor(name, shape, dt))

        def sem(name):
            return ctx.enter_context(nc.semaphore(name))

        ident = sb("ident", [P, P])
        vec_rows = sb("vec_rows", [5 + NH, C])
        vec_cols = sb("vec_cols", [P, 2, 5])
        b_in_col = sb("b_in_col", [P, NH])
        wu = sb("wu", [P, 2, 2])
        bias_qkv = sb("bias_qkv", [P, QKV])
        bias_half = sb("bias_half", [P, QKV])
        bias_kf = sb("bias_kf", [P, NH])
        minus_half = sb("minus_half", [P, 2 * NT])
        qkv_w = sb("qkv_w", [P, 4, QKV * P], F32R)
        kf_w = sb("kf_w", [P, 4, HID], F32R)
        in_w = sb("in_w", [P, 4, HID], F32R)
        rf_w = sb("rf_w", [P, 4, C], F32R)
        rf_bias = sb("rf_bias", [P, C], F32R)
        rf_pick = sb("rf_pick", [P, P], F32R)
        wo_a = sb("wo_a", [P, C])
        wo_b = sb("wo_b", [P, 2, C])
        vf_w = sb("vf_w", [P, NH, C])
        out_w = sb("out_w", [P, NH, C])
        ids = sb("ids", [P, B, NT], I32)
        id_f = sb("id_f", [P, B, NT])
        id_ok = sb("id_ok", [P, B, NT])
        rows = sb("rows", [P, B * NT], U32)

        h0 = sb("h0", [P, H0_SLOTS, 2, NT, C])
        resid = sb("resid", [P, 2, NT, C])
        gate = sb("gate", [P, 2, NT, C])
        normed = sb("normed", [P, 2, NT, C])
        NE = len(norms)
        stats = sb("stats", [P, 2, NT, 6])
        mean_var = sb("mean_var", [P, NE, NT, 2])
        var_arg = sb("var_arg", [P, NE, 2, NT])
        rstd = sb("rstd", [P, NE, 2, NT])
        shift = sb("shift", [P, NE, 2, NT])

        act_a = sb("act_a", [P, 2, 2, T], F32R)
        act_b = sb("act_b", [P, 2, T], F32R)
        key = sb("key", [P, 2, 3, T])
        val = sb("val", [P, 2, 3, T])
        rec = sb("rec", [P, 2, 3, T])
        mixed = sb("mixed", [P, 3, T])
        mx = sb("mx", [P, 2 * (T + 1)])
        ex = sb("ex", [P, 4, T])
        ev = sb("ev", [P, 2, T])
        st = sb("st", [P, 4, T])
        wt = sb("wt", [P, 2, 2, T])
        cen = sb("cen", [P, 2, T])
        hid = sb("hid", [P, 2, NH, T])

        spare = hid[:].rearrange("p q m t -> p (q m t)")
        taken = [0]

        def stage(m, c):
            at = taken[0]
            taken[0] += m * c
            return spare[:, at:at + m * c].rearrange("p (m c) -> p m c", c=c)

        nat_qkv = stage(QKV, C)
        nat_wo = stage(2, C)
        nat_rf = stage(2, C)
        nat_rf_t = stage(2, C)
        ln2b_rep = stage(2, P)
        nat_kf = stage(NH, C)
        nat_in = stage(NH, C)
        ln1b_all = stage(1, C)[:, 0]
        ln2b_all = stage(1, C)[:, 0]
        rf_bias_h = stage(1, C)[:, 0]
        junk = stage(1, C)[:, 0]
        assert taken[0] <= 2 * NH * T
        nat_vf = gate[:].rearrange("p q j c -> p (q j c)").rearrange("p (m c) -> p m c", c=HID)

        ps_t = ctx.enter_context(nc.psum_tensor("ps_t", [P, 2, T], F32))
        ps_c = ctx.enter_context(nc.psum_tensor("ps_c", [P, 4, T], F32))
        ps_o = ctx.enter_context(nc.psum_tensor("ps_o", [P, 2, 512], F32))
        RING = 4

        ids_in = sem("ids_in")
        vecs_in = sem("vecs_in")
        lnb_in = sem("lnb_in")
        nat_qkv_in = sem("nat_qkv_in")
        nat_wo_in = sem("nat_wo_in")
        nat_rf_in = sem("nat_rf_in")
        nat_kf_in = sem("nat_kf_in")
        nat_in_in = sem("nat_in_in")
        nat_vf_in = sem("nat_vf_in")
        out_w_in = sem("out_w_in")
        mix_halves_in = sem("mix_halves_in")
        ffn_halves_in = sem("ffn_halves_in")
        gathered = [sem(f"gathered{b}") for b in range(B)]
        out_stored = [sem(f"out_stored{q}") for q in range(2)]
        consts = sem("consts")
        h0_cleared = sem("h0_cleared")
        rows_ready = sem("rows_ready")
        edges_ready = sem("edges_ready")
        prep_filled = sem("prep_filled")
        prep_high = sem("prep_high")
        prep_low = sem("prep_low")
        cols_ready = sem("cols_ready")
        bias_ready = sem("bias_ready")
        var_ready = sem("var_ready")
        rstd_ready = sem("rstd_ready")
        shift_ready = sem("shift_ready")
        normed_ready = sem("normed_ready")
        x0_ready = sem("x0_ready")
        res_ready = sem("res_ready")
        h1_ready = sem("h1_ready")
        t_filled = sem("t_filled")
        high_ready = sem("high_ready")
        low_ready = sem("low_ready")
        c_filled = sem("c_filled")
        c_freed = sem("c_freed")
        even_ready = sem("even_ready")
        odd_ready = sem("odd_ready")
        o_filled = sem("o_filled")
        o_freed = sem("o_freed")
        d_ready = sem("d_ready")
        e_ready = sem("e_ready")
        ev_ready = sem("ev_ready")
        w_arg = sem("w_arg")
        w_ready = sem("w_ready")
        ecv_ready = sem("ecv_ready")
        st_ready = sem("st_ready")
        sw_ready = sem("sw_ready")
        sum_ready = sem("sum_ready")
        rden_ready = sem("rden_ready")
        z_ready = sem("z_ready")
        act_step = sem("act_step")
        dve_step = sem("dve_step")
        pool_step = sem("pool_step")

        prep = []
        for m in range(0, QKV, 2):
            prep.append(("split", qkv_w, nat_qkv, m, [P] * min(2, QKV - m), 0))
        prep.append(("wo", None, nat_wo, 0, [P, CB], None))
        prep.append(("rf", rf_w, nat_rf, 0, [P, CB], 1))
        for m in range(0, NH, 2):
            prep.append(("split", kf_w, nat_kf, m, [P, P], 1))
        for m in range(0, NH, 2):
            prep.append(("vf", None, nat_vf, m, [P, P], None))
        for m in range(0, NH, 2):
            prep.append(("split", in_w, nat_in, m, [P, P], None))
        SPLIT_W = {id(qkv_w): nat_qkv_in, id(kf_w): nat_kf_in, id(in_w): nat_in_in}
        PREPS = len(prep) + 2

        def prep_bank(n):
            return ps_c[:, n + 1] if n < 3 else ps_o[:, (n - 3) % 2]

        def splits(k):
            return sum(item[0] in ("split", "rf") for item in prep[:k])

        block = ctx.enter_context(nc.Block())

        @block.sync
        def _(sp):
            sp.dma_start(ids[:], x.rearrange("b (p j) -> p b j", j=NT)).then_inc(ids_in, 16)
            for n, v in enumerate((ln1_w, ln2_w, decay, first, ln2_b)):
                sp.dma_start(vec_rows[n:n + 1, :], v.rearrange("(a c) -> a c", a=1)).then_inc(vecs_in, 16)
            sp.dma_start(vec_rows[5:5 + NH, 0:P], b_in.rearrange("(a c) -> a c", c=P)).then_inc(vecs_in, 16)
            for m, w in enumerate((Wk, Wv, Wr)):
                sp.dma_start(nat_qkv[:, m, :], w[0:P, :]).then_inc(nat_qkv_in, 16)
            for m, half, w in ((3, 0, Wk), (3, 1, Wv), (4, 0, Wr), (4, 1, Wr)):
                sp.dma_start(nat_qkv[64 * half:64 * half + 64, m, :], w[P:C, :]).then_inc(nat_qkv_in, 16)
            sp.dma_start(ln1b_all, ln1_b.partition_broadcast(P)).then_inc(lnb_in, 16)
            sp.dma_start(ln2b_all, ln2_b.partition_broadcast(P)).then_inc(lnb_in, 16)
            for w, nat, s in ((Wo, nat_wo, nat_wo_in), (Wrf, nat_rf, nat_rf_in)):
                sp.dma_start(nat[:, 0, :], w[0:P, :]).then_inc(s, 16)
                sp.dma_start(nat[0:CB, 1, :], w[P:C, :]).then_inc(s, 16)
            sp.dma_start(nat_kf, Wkf.rearrange("(m p) c -> p m c", p=P)).then_inc(nat_kf_in, 16)
            sp.dma_start(nat_vf[:, 0, :], Wvf[0:P, :]).then_inc(nat_vf_in, 16)
            sp.dma_start(nat_vf[0:CB, 1, :], Wvf[P:C, :]).then_inc(nat_vf_in, 16)
            sp.dma_start(nat_in, w_in.rearrange("(m p) c -> p m c", p=P)).then_inc(nat_in_in, 16)
            sp.dma_start(out_w[:], w_out.rearrange("(m p) c -> p m c", p=P)).then_inc(out_w_in, 16)
            for items, w, copied in ((8, rf_w, mix_halves_in), (8, kf_w, mix_halves_in),
                                     (len(prep), in_w, ffn_halves_in)):
                sp.wait_ge(prep_low, splits(items))
                sp.dma_start(w[0:64, 2:4, :].bitcast(F32), w[64:128, 2:4, :].bitcast(F32)).then_inc(copied, 16)
            for p in range(PAIRS):
                for q in range(2):
                    sp.wait_ge(o_freed, out_no["ffn", p, q] + 2)
                    sp.dma_start(out[2 * p + q].rearrange("(p j) c -> p (j c)", j=NT),
                                 resid[:, q].rearrange("p j c -> p (j c)")).then_inc(out_stored[q], 16)
            for q in range(2):
                sp.wait_ge(out_stored[q], 16 * PAIRS)

        @block.gpsimd
        def _(pool):
            g = nc.gpsimd
            g.memset(ident[:], 0.0).then_inc(pool_step, 1)
            pool.wait_ge(pool_step, 1)
            g.affine_select(out=ident[:], in_=ident[:], compare_op=ALU.not_equal, fill=1.0, base=0,
                            pattern=[[-1, P]], channel_multiplier=1).then_inc(consts, 1)
            g.memset(minus_half[:], -0.5).then_inc(consts, 1)

            def clear_rows(p):
                if p >= H0_SLOTS:
                    pool.wait_ge(res_ready, 2 * (p - H0_SLOTS) + 2)
                g.memset(h0[:, p % H0_SLOTS], 0.0).then_inc(h0_cleared, 1)

            def gather(p, q):
                b = 2 * p + q
                pool.wait_ge(h0_cleared, p + 1)
                if b == 0:
                    pool.wait_ge(rows_ready, 1)
                for j in range(NT):
                    g.indirect_dma_start(
                        out=h0[:, p % H0_SLOTS, q, j, :], out_offset=None, in_=table,
                        in_offset=bass.IndirectOffsetOnAxis(ap=rows[:, b * NT + j:b * NT + j + 1], axis=0),
                        bounds_check=VOCAB - 1, oob_is_err=False).then_inc(gathered[b], 16)

            def inv_sqrt(kind, p, q):
                e = norm_no[kind, p, q]
                k = 2 if kind == "qkv" else 1
                if e == 0:
                    pool.wait_ge(consts, 2)
                pool.wait_ge(var_ready, e + 1)
                g.tensor_tensor(rstd[:, e, 0:k, :].rearrange("p k j -> p (k j)"),
                                var_arg[:, e, 0:k, :].rearrange("p k j -> p (k j)"),
                                minus_half[:, 0:k * NT], ALU.pow).then_inc(rstd_ready, 1)

            def first_residual(p, q):
                e = norm_no["qkv", p, q]
                pool.wait_ge(shift_ready, e + 1)
                if p:
                    pool.wait_ge(out_stored[q], 16 * p)
                for j in range(NT):
                    ins = g.tensor_scalar(resid[:, q, j, :], h0[:, p % H0_SLOTS, q, j, :],
                                          rstd[:, e, 0, j:j + 1], shift[:, e, 0, j:j + 1], ALU.mult, ALU.add)
                ins.then_inc(x0_ready, 1)

            def second_residual(p, q):
                pool.wait_ge(normed_ready, norm_no["mix", p, q] + 1)
                r = resid[:, q].rearrange("p j c -> p (j c)")
                g.tensor_tensor(r, r, h0[:, p % H0_SLOTS, q].rearrange("p j c -> p (j c)"),
                                ALU.add).then_inc(res_ready, 1)

            def weigh_values(p, j):
                t = tile_no(p, j)
                pool.wait_ge(e_ready, 2 * t + 2)
                if t:
                    pool.wait_ge(st_ready, 4 * t)
                pool.wait_ge(c_freed, taken_to("value", p, j))
                v = val[:, p % 2, j, :].unsqueeze(1).to_broadcast([P, 2, T])
                g.tensor_tensor(ev[:], ex[:, 2:4, :], v, ALU.mult).then_inc(ev_ready, 1)

            def weigh_centre(p, j):
                t = tile_no(p, j)
                pool.wait_ge(w_ready, 2 * t + 2)
                g.tensor_tensor(cen[:, 0, :], cen[:, 1, :], val[:, p % 2, j, :],
                                ALU.mult).then_inc(ecv_ready, 1)

            def weigh_states(p, j, *parts):
                t = tile_no(p, j)
                for n in parts or (0, 1):
                    pool.wait_ge(st_ready, 4 * t + 2 * n + 2)
                    s = st[:, 2 * n:2 * n + 2, :]
                    g.tensor_tensor(s, s, wt[:, t % 2], ALU.mult).then_inc(sw_ready, 1)

            def square(p, q):
                n = chunk_start("mix", p, q)
                for m in range(0, NH, 2):
                    pool.wait_ge(c_freed, n + m + 1)
                    h = hid[:, q, m, :]
                    g.tensor_tensor(h, h, h, ALU.mult).then_inc(even_ready, 1)

            clear_rows(0)
            gather(0, 0)
            gather(0, 1)
            inv_sqrt("qkv", 0, 0)
            inv_sqrt("qkv", 0, 1)
            clear_rows(1)
            clear_rows(2)
            gather(1, 0)
            gather(1, 1)
            weigh_values(0, 0)
            weigh_centre(0, 0)
            weigh_states(0, 0)
            inv_sqrt("qkv", 1, 0)
            weigh_values(0, 2)
            inv_sqrt("qkv", 1, 1)
            gather(2, 0)
            weigh_centre(0, 2)
            weigh_states(0, 2)
            gather(2, 1)
            first_residual(0, 0)
            weigh_values(0, 1)
            weigh_centre(0, 1)
            inv_sqrt("qkv", 2, 0)
            inv_sqrt("qkv", 2, 1)
            weigh_states(0, 1)
            inv_sqrt("mix", 0, 0)
            for s in range(1, PAIRS + 1):
                mix, wkv, nxt = s - 1, s, s + 2
                first_residual(mix, 1)
                second_residual(mix, 0)
                inv_sqrt("mix", mix, 1)
                if has(wkv):
                    weigh_values(wkv, 0)
                    weigh_centre(wkv, 0)
                    weigh_states(wkv, 0)
                second_residual(mix, 1)
                if has(wkv):
                    weigh_values(wkv, 2)
                square(mix, 0)
                if has(wkv):
                    weigh_centre(wkv, 2)
                    weigh_states(wkv, 2)
                square(mix, 1)
                inv_sqrt("ffn", mix, 0)
                if has(wkv):
                    weigh_values(wkv, 1)
                if has(nxt) and nxt >= H0_SLOTS:
                    clear_rows(nxt)
                if has(wkv):
                    weigh_centre(wkv, 1)
                inv_sqrt("ffn", mix, 1)
                if has(wkv):
                    weigh_states(wkv, 1)
                if has(nxt):
                    if nxt >= H0_SLOTS:
                        gather(nxt, 0)
                        gather(nxt, 1)
                    inv_sqrt("qkv", nxt, 0)
                    inv_sqrt("qkv", nxt, 1)
                if has(wkv):
                    first_residual(wkv, 0)
                    inv_sqrt("mix", wkv, 0)

        @block.scalar
        def _(act):
            a = nc.scalar
            own = [0]

            def after(ins):
                own[0] += 1
                ins.then_inc(act_step, 1)
                act.wait_ge(act_step, own[0])

            def prepare(first_item, last_item):
                for n, (kind, dst, nat, m, sizes, ln) in list(enumerate(prep))[first_item:last_item]:
                    bank = prep_bank(n)
                    if n == 0:
                        act.wait_ge(cols_ready, 5)
                    act.wait_ge(prep_filled, n + 2)
                    cols = sum(sizes)
                    if kind == "split" or kind == "rf":
                        if kind == "rf":
                            a.activation(nat_rf_t[:, 0, :], bank[:, 0:C], ACT.Identity).then_inc(act_step, 1)
                            a.activation(nat_rf_t[:, 1, :], bank[:, 256:256 + C], ACT.Identity).then_inc(act_step, 1)
                            own[0] += 2
                        at = m * P
                        scale_a = 1.0 if ln is None else vec_cols[:, 0, ln:ln + 1]
                        scale_b = 1.0 if ln is None else vec_cols[64:128, 1, ln:ln + 1]
                        a.activation(dst[:, 0, at:at + cols], bank[:, 0:cols], ACT.Identity, scale=scale_a)\
                            .then_inc(act_step, 1)
                        own[0] += 1
                        if n < 3:
                            a.activation(dst[0:64, 2, at:at + cols], bank[64:128, 256:256 + cols],
                                         ACT.Identity, scale=scale_b).then_inc(act_step, 1)
                            own[0] += 1
                        a.activation(dst[64:128, 2, at:at + cols], bank[64:128, 256:256 + cols],
                                     ACT.Identity, scale=scale_b).then_inc(prep_high, 1)
                    elif kind == "wo":
                        a.activation(wo_a[:], bank[:, 0:C], ACT.Identity, scale=0.5).then_inc(act_step, 1)
                        own[0] += 1
                        act.wait_ge(edges_ready, 3)
                        a.activation(wo_b[0:64, 0, :], bank[64:128, 256:256 + C], ACT.Identity, scale=0.5)\
                            .then_inc(act_step, 1)
                        own[0] += 1
                        a.activation(wo_b[64:128, 1, :], bank[64:128, 256:256 + C], ACT.Identity, scale=0.5)\
                            .then_inc(prep_high, 1)
                    else:
                        a.activation(vf_w[:, m:m + 2, :], bank[:, 0:2 * C].rearrange("p (m c) -> p m c", c=C),
                                     ACT.Identity, scale=0.5).then_inc(prep_high, 1)

            def round_high(kind, p, q):
                e = norm_no[kind, p, q]
                act.wait_ge(t_filled, e + 1)
                if e >= 2:
                    act.wait_ge(c_filled, chunks_to[e - 2])
                a.activation(act_a[:, e % 2, 0, :], ps_t[:, 0], ACT.Identity).then_inc(high_ready, 1)
                a.activation(act_b[64:128, e % 2, :], ps_t[64:128, 1], ACT.Identity).then_inc(high_ready, 1)

            def take_qkv(p, q):
                n, slot = chunk_start("qkv", p, q), p % 2
                if p >= 2:
                    act.wait_ge(z_ready, 3 * (p - 1))
                bank = [ps_c[:, (n + i) % RING] for i in range(QKV)]
                act.wait_ge(c_filled, n + 1)
                if n == 0:
                    act.wait_ge(bias_ready, 1)
                a.activation(key[:, slot, q, :], bank[0], ACT.Identity, bias=bias_qkv[:, 0:1]).then_inc(c_freed, 1)
                act.wait_ge(c_filled, n + 2)
                a.activation(val[:, slot, q, :], bank[1], ACT.Identity, bias=bias_qkv[:, 1:2]).then_inc(c_freed, 1)
                act.wait_ge(c_filled, n + 3)
                a.activation(rec[:, slot, q, :], bank[2], ACT.Tanh, bias=bias_half[:, 2:3], scale=0.5)\
                    .then_inc(c_freed, 1)
                act.wait_ge(c_filled, n + 4)
                mine = slice(64 * q, 64 * q + 64)
                own[0] += 1
                a.activation(key[mine, slot, 2, :], bank[3][0:64], ACT.Identity, bias=bias_qkv[0:64, 3:4])\
                    .then_inc(act_step, 1)
                a.activation(val[mine, slot, 2, :], bank[3][64:128], ACT.Identity, bias=bias_qkv[64:128, 3:4])\
                    .then_inc(c_freed, 1)
                act.wait_ge(c_filled, n + 5)
                a.activation(rec[mine, slot, 2, :], bank[4][mine], ACT.Tanh, bias=bias_half[mine, 4:5], scale=0.5)\
                    .then_inc(c_freed, 1)

            def exp_steps(p, j):
                t, part = tile_no(p, j), j // 2
                act.wait_ge(d_ready, 2 * t + 1)
                a.activation(ex[:, 0:2, :], ex[:, 0:2, :], ACT.Exp, bias=wu[:, part, 0:1]).then_inc(e_ready, 1)
                act.wait_ge(d_ready, 2 * t + 2)
                a.activation(ex[:, 2:4, :], ex[:, 2:4, :], ACT.Exp).then_inc(e_ready, 1)

            def exp_weights(p, j):
                t, part = tile_no(p, j), j // 2
                act.wait_ge(w_arg, 2 * t + 1)
                a.activation(wt[:, t % 2], wt[:, t % 2], ACT.Exp).then_inc(w_ready, 1)
                act.wait_ge(w_arg, 2 * t + 2)
                a.activation(cen[:, 1, :], cen[:, 1, :], ACT.Exp, bias=wu[:, part, 1:2])\
                    .then_inc(w_ready, 1)

            def invert(p, j):
                t = tile_no(p, j)
                act.wait_ge(sum_ready, t + 1)
                d = wt[:, t % 2, 1, :]
                after(a.activation(d, d, ACT.Ln))
                a.activation(d, d, ACT.Exp, scale=-1.0).then_inc(rden_ready, 1)

            def take_mix(p, q, chunks=range(NH)):
                n = chunk_start("mix", p, q)
                if p and 0 in chunks:
                    act.wait_ge(o_filled, out_no["ffn", p - 1, q] + 2)
                for m in chunks:
                    act.wait_ge(c_filled, n + m + 1)
                    a.activation(hid[:, q, m, :], ps_c[:, (n + m) % RING], ACT.Relu, bias=bias_kf[:, m:m + 1])\
                        .then_inc(c_freed, 1)

            def take_gate(p, q, h):
                n = chunk_start("mix", p, q)
                if p and h == 0:
                    act.wait_ge(h1_ready, 2 * p + q - 1)
                act.wait_ge(c_filled, n + NH + h + 1)
                a.activation(gate[:, q, 2 * h:2 * h + 2, :].rearrange("p j c -> p (j c)"),
                             ps_c[:, (n + NH + h) % RING, 0:2 * C], ACT.Tanh, scale=0.5).then_inc(c_freed, 1)

            def take_ffn(p, q):
                n = chunk_start("ffn", p, q)
                act.wait_ge(o_filled, out_no["chan", p, q] + 2)
                for m in range(NH):
                    act.wait_ge(c_filled, n + m + 1)
                    a.activation(hid[:, q, m, :], ps_c[:, (n + m) % RING], ACT.Gelu, bias=b_in_col[:, m:m + 1])\
                        .then_inc(c_freed, 1)

            prepare(0, 5)
            round_high("qkv", 0, 0)
            take_qkv(0, 0)
            round_high("qkv", 0, 1)
            exp_steps(0, 0)
            prepare(5, 7)
            exp_weights(0, 0)
            take_qkv(0, 1)
            prepare(7, 9)
            exp_steps(0, 2)
            invert(0, 0)
            round_high("qkv", 1, 0)
            exp_weights(0, 2)
            take_qkv(1, 0)
            prepare(9, 11)
            round_high("qkv", 1, 1)
            exp_steps(0, 1)
            prepare(11, len(prep) - 1)
            take_qkv(1, 1)
            prepare(len(prep) - 1, len(prep))
            invert(0, 2)
            act.wait_ge(prep_filled, PREPS)
            bank = prep_bank(len(prep))
            a.activation(rf_bias[0:1, :], bank[0:1, 0:C], ACT.Identity).then_inc(act_step, 1)
            own[0] += 1
            a.activation(rf_bias_h[32:33, :].bitcast(F32R), bank[32:33, 0:C], ACT.Identity)\
                .then_inc(prep_high, 1)
            exp_weights(0, 1)
            round_high("qkv", 2, 0)
            invert(0, 1)
            for s in range(1, PAIRS + 1):
                mix, wkv, prj, nxt = s - 1, s, s + 1, s + 2
                if has(prj):
                    round_high("qkv", prj, 1)
                    take_qkv(prj, 0)
                else:
                    round_high("mix", mix, 0)
                if has(wkv):
                    exp_steps(wkv, 0)
                if has(prj):
                    round_high("mix", mix, 0)
                    take_qkv(prj, 1)
                if has(wkv) and has(prj):
                    exp_weights(wkv, 0)
                if has(prj):
                    round_high("mix", mix, 1)
                if mix == 0:
                    act.wait_ge(bias_ready, 3)
                take_mix(mix, 0, range(3))
                if has(wkv) and not has(prj):
                    exp_weights(wkv, 0)
                take_mix(mix, 0, range(3, NH))
                if not has(prj):
                    round_high("mix", mix, 1)
                if has(wkv):
                    exp_steps(wkv, 2)
                take_gate(mix, 0, 0)
                take_gate(mix, 0, 1)
                take_mix(mix, 1, range(2))
                if has(wkv):
                    invert(wkv, 0)
                    exp_weights(wkv, 2)
                take_mix(mix, 1, range(2, NH))
                if has(wkv):
                    exp_steps(wkv, 1)
                take_gate(mix, 1, 0)
                take_gate(mix, 1, 1)
                if has(wkv):
                    invert(wkv, 2)
                round_high("ffn", mix, 0)
                if has(wkv):
                    exp_weights(wkv, 1)
                take_ffn(mix, 0)
                if has(wkv):
                    invert(wkv, 1)
                round_high("ffn", mix, 1)
                take_ffn(mix, 1)
                if has(nxt):
                    round_high("qkv", nxt, 0)

        @block.vector
        def _(dve):
            v = nc.vector
            own = [0]

            def step(ins):
                own[0] += 1
                ins.then_inc(dve_step, 1)
                return own[0]

            def after(ins):
                dve.wait_ge(dve_step, step(ins))

            def set_up():
                dve.wait_ge(ids_in, 16)
                after(v.tensor_scalar(id_ok[:], ids[:], 0.0, None, ALU.is_ge))
                after(v.scalar_tensor_tensor(id_ok[:], ids[:], float(VOCAB), id_ok[:], ALU.is_lt, ALU.mult))
                after(v.scalar_tensor_tensor(id_f[:], ids[:], -float(VOCAB), id_ok[:], ALU.add, ALU.mult))
                v.tensor_scalar(rows[:], id_f[:].rearrange("p b j -> p (b j)"), float(VOCAB), None, ALU.add)\
                    .then_inc(rows_ready, 1)
                dve.wait_ge(prep_filled, 1)
                bank = ps_c[:, 0]
                v.tensor_copy(vec_cols[:, 0, :], bank[:, 0:5]).then_inc(cols_ready, 1)
                v.tensor_copy(vec_cols[64:128, 1, :], bank[64:128, 16:21]).then_inc(cols_ready, 1)
                v.tensor_copy(vec_cols[0:64, 1, :], bank[64:128, 16:21]).then_inc(cols_ready, 1)
                v.tensor_copy(b_in_col[:], bank[:, 5:5 + NH]).then_inc(cols_ready, 1)
                dve.wait_ge(cols_ready, 4)
                v.tensor_scalar(wu[:], vec_cols[:, :, 2:4], 1.0 / T, None, ALU.mult).then_inc(cols_ready, 1)

            def set_edges():
                step(v.memset(mx[:, 0:1], M_START))
                step(v.memset(mx[:, 2 * T + 1:2 * T + 2], M_START))
                for n, edge in ((0, 0), (1, T - 1), (2, 0), (3, T - 1)):
                    step(v.memset(st[:, n, edge:edge + 1], 0.0))
                v.memset(wo_b[:], 0.0).then_inc(edges_ready, 1)
                v.memset(rf_bias[:].bitcast(F32), 0.0).then_inc(edges_ready, 1)
                v.memset(rf_pick[:].bitcast(F32), 0.0).then_inc(edges_ready, 1)
                dve.wait_ge(edges_ready, 3)
                step(v.memset(rf_pick[0:1, :].bitcast(F32), 1.0))
                step(v.memset(rf_pick[32:33, :].bitcast(F32), 1.0))

            def fold_bias(bias, w, lnb, m):
                after(v.scalar_tensor_tensor(junk, w[:, m, :], 1.0, lnb, ALU.mult, ALU.mult,
                                             accum_out=bias[:, m:m + 1]))

            def prepare(first_item, last_item):
                for n, (kind, dst, nat, m, sizes, ln) in list(enumerate(prep))[first_item:last_item]:
                    bank = prep_bank(n)
                    if kind not in ("split", "rf"):
                        continue
                    dve.wait_ge(prep_high, n + 1)
                    cols, at = sum(sizes), m * P
                    scale_a = 1.0 if ln is None else vec_cols[:, 0, ln:ln + 1]
                    scale_b = 1.0 if ln is None else vec_cols[64:128, 1, ln:ln + 1]
                    step(v.scalar_tensor_tensor(dst[:, 1, at:at + cols], bank[:, 0:cols], scale_a,
                                                dst[:, 0, at:at + cols].bitcast(F32), ALU.mult, ALU.subtract))
                    for half in (1, 0) if n < 3 else (0,):
                        rows_out = slice(0, 64) if half else slice(64, 128)
                        ins = v.scalar_tensor_tensor(dst[rows_out, 3, at:at + cols],
                                                     bank[64:128, 256:256 + cols], scale_b,
                                                     dst[64:128, 2, at:at + cols].bitcast(F32),
                                                     ALU.mult, ALU.subtract)
                        if half:
                            step(ins)
                    ins.then_inc(prep_low, 1)

            def statistics(kind, p, q, src):
                e = norm_no[kind, p, q]
                for j in range(NT):
                    done = step(v.bn_stats(stats[:, e % 2, j, :], src[:, j, :]))
                for j in range(NT):
                    dve.wait_ge(dve_step, done - NT + 1 + j)
                    last = step(v.bn_aggr(mean_var[:, e, j, :], stats[:, e % 2, j, :]))
                dve.wait_ge(dve_step, last)
                var = mean_var[:, e, :, 1]
                if kind == "qkv":
                    step(v.tensor_scalar(var_arg[:, e, 1, :], var, 1.0 + EPS, EPS * EPS, ALU.mult, ALU.add))
                v.tensor_scalar(var_arg[:, e, 0, :], var, EPS, None, ALU.add).then_inc(var_ready, 1)

            def normalise(kind, p, q, src):
                e = norm_no[kind, p, q]
                k = 2 if kind == "qkv" else 1
                dve.wait_ge(rstd_ready, e + 1)
                mean = mean_var[:, e, :, 0].unsqueeze(1).to_broadcast([P, k, NT])
                v.scalar_tensor_tensor(shift[:, e, 0:k, :], mean, -1.0, rstd[:, e, 0:k, :],
                                       ALU.mult, ALU.mult).then_inc(shift_ready, 1)
                dve.wait_ge(shift_ready, e + 1)
                if e >= 2:
                    dve.wait_ge(t_filled, e - 1)
                for j in range(NT):
                    ins = v.tensor_scalar(normed[:, e % 2, j, :], src[:, j, :], rstd[:, e, k - 1, j:j + 1],
                                          shift[:, e, k - 1, j:j + 1], ALU.mult, ALU.add)
                    if j < NT - 1:
                        step(ins)
                ins.then_inc(normed_ready, 1)

            def embed_statistics(p, q):
                dve.wait_ge(gathered[2 * p + q], 16 * NT)
                statistics("qkv", p, q, h0[:, p % H0_SLOTS, q])

            def embed_normalise(p, q):
                normalise("qkv", p, q, h0[:, p % H0_SLOTS, q])

            def split_low(kind, p, q):
                e = norm_no[kind, p, q]
                dve.wait_ge(high_ready, 2 * e + 1)
                v.tensor_tensor(act_a[:, e % 2, 1, :], ps_t[:, 0], act_a[:, e % 2, 0, :].bitcast(F32),
                                ALU.subtract).then_inc(low_ready, 1)
                dve.wait_ge(high_ready, 2 * e + 2)
                v.tensor_tensor(act_b[0:64, e % 2, :], ps_t[64:128, 1], act_b[64:128, e % 2, :].bitcast(F32),
                                ALU.subtract).then_inc(low_ready, 1)

            mx_excl = bass.AP(mx, 0, [[2 * (T + 1), P], [T + 2, 2], [1, T]])
            mx_incl = bass.AP(mx, 1, [[2 * (T + 1), P], [T, 2], [1, T]])
            mx_b = mx[:, T + 1:2 * T + 2]

            def maxima(p, j):
                t, part, k = tile_no(p, j), j // 2, key[:, p % 2, j, :]
                w = wu[:, part, 0:1].to_broadcast([P, T])
                dve.wait_ge(c_freed, taken_to("key", p, j))
                if t:
                    dve.wait_ge(w_arg, 2 * t - 1)
                step(v.tensor_tensor_scan(mx[:, 1:T + 1], w, k, M_START, ALU.add, ALU.max))
                done = step(v.tensor_tensor_scan(bass.AP(mx, 2 * T, [[2 * (T + 1), P], [-1, T]]),
                                                 w, bass.AP(key, ((p % 2) * 3 + j) * T + T - 1, [[6 * T, P], [-1, T]]),
                                                 M_START, ALU.add, ALU.max))
                dve.wait_ge(dve_step, done)
                v.tensor_tensor(ex[:, 0:2, :], mx_excl, mx_incl, ALU.subtract).then_inc(d_ready, 1)
                v.tensor_tensor(ex[:, 2:4, :], k.unsqueeze(1).to_broadcast([P, 2, T]), mx_incl, ALU.subtract)\
                    .then_inc(d_ready, 1)

            def common_max(p, j):
                t, part, k = tile_no(p, j), j // 2, key[:, p % 2, j, :]
                m = cen[:, 0, :]
                if t:
                    dve.wait_ge(sum_ready, t)
                if t >= 2:
                    dve.wait_ge(z_ready, t - 1)
                after(v.tensor_tensor(m, mx[:, 0:T], mx_b[:, 1:T + 1], ALU.max))
                after(v.scalar_tensor_tensor(m, k, wu[:, part, 1:2], m, ALU.add, ALU.max))
                v.tensor_tensor(wt[:, t % 2], mx_excl, m.unsqueeze(1).to_broadcast([P, 2, T]), ALU.subtract)\
                    .then_inc(w_arg, 1)
                v.tensor_tensor(cen[:, 1, :], k, m, ALU.subtract).then_inc(w_arg, 1)

            def back(tile, offset, count):
                return bass.AP(tile[:].tensor, offset, [[tile[:].ap[0][0], P], [-1, count]])

            def scans(p, j):
                t = tile_no(p, j)
                for n, (data, base) in enumerate(((ev, 0), (ex, 2 * T))):
                    if n == 0:
                        dve.wait_ge(ev_ready, t + 1)
                    src = ev[:, 0, :] if n == 0 else ex[:, 2, :]
                    v.tensor_tensor_scan(st[:, 2 * n, 1:T], ex[:, 0, 0:T - 1], src[:, 0:T - 1], 0.0,
                                         ALU.mult, ALU.add).then_inc(st_ready, 1)
                    v.tensor_tensor_scan(back(st, (2 * n + 1) * T + T - 2, T - 1),
                                         back(ex, T + T - 1, T - 1), back(data, base + T + T - 1, T - 1), 0.0,
                                         ALU.mult, ALU.add).then_inc(st_ready, 1)

            def sums(p, j):
                t = tile_no(p, j)
                dve.wait_ge(sw_ready, 2 * t + 2)
                dve.wait_ge(ecv_ready, t + 1)
                s = st[:].rearrange("p (n d) t -> p n d t", d=2)
                after(v.tensor_tensor(wt[:, t % 2], s[:, :, 0, :], s[:, :, 1, :], ALU.add))
                v.tensor_tensor(wt[:, t % 2], wt[:, t % 2], cen[:], ALU.add).then_inc(sum_ready, 1)

            def gated(p, j):
                t = tile_no(p, j)
                dve.wait_ge(rden_ready, t + 1)
                dve.wait_ge(c_freed, taken_to("receptance", p, j))
                y, r = wt[:, t % 2, 0, :], rec[:, p % 2, j, :]
                after(v.tensor_tensor(y, y, wt[:, t % 2, 1, :], ALU.mult))
                if p:
                    dve.wait_ge(o_filled, out_no["attn", p - 1, min(j, 1)] + 2)
                v.scalar_tensor_tensor(mixed[:, j, :], r, 1.0, y, ALU.add, ALU.mult).then_inc(z_ready, 1)

            def add_attention(p, q):
                n = out_no["attn", p, q]
                dve.wait_ge(x0_ready, 2 * p + q + 1)
                for h in range(2):
                    dve.wait_ge(o_filled, n + h + 1)
                    r = resid[:, q, 2 * h:2 * h + 2, :].rearrange("p j c -> p (j c)")
                    v.tensor_tensor(r, ps_o[:, h, 0:2 * C], r, ALU.add).then_inc(o_freed, 1)
                dve.wait_ge(o_freed, n + 2)
                statistics("mix", p, q, resid[:, q])

            def square(p, q):
                n = chunk_start("mix", p, q)
                for m in range(1, NH, 2):
                    dve.wait_ge(c_freed, n + m + 1)
                    h = hid[:, q, m, :]
                    v.tensor_tensor(h, h, h, ALU.mult).then_inc(odd_ready, 1)

            def add_channel_mix(p, q):
                n = out_no["chan", p, q]
                dve.wait_ge(c_freed, chunk_end("mix", p, q))
                for h in range(2):
                    dve.wait_ge(o_filled, n + h + 1)
                    g = gate[:, q, 2 * h:2 * h + 2, :].rearrange("p j c -> p (j c)")
                    v.scalar_tensor_tensor(g, g, 1.0, ps_o[:, h, 0:2 * C], ALU.add, ALU.mult).then_inc(o_freed, 1)
                dve.wait_ge(o_freed, n + 2)
                dve.wait_ge(res_ready, 2 * p + q + 1)
                r = resid[:, q].rearrange("p j c -> p (j c)")
                v.tensor_tensor(r, r, gate[:, q].rearrange("p j c -> p (j c)"), ALU.add).then_inc(h1_ready, 1)
                dve.wait_ge(h1_ready, 2 * p + q + 1)
                statistics("ffn", p, q, resid[:, q])

            def add_ffn(p, q):
                n = out_no["ffn", p, q]
                for h in range(2):
                    dve.wait_ge(o_filled, n + h + 1)
                    r = resid[:, q, 2 * h:2 * h + 2, :].rearrange("p j c -> p (j c)")
                    v.tensor_tensor(r, ps_o[:, h, 0:2 * C], r, ALU.add).then_inc(o_freed, 1)

            def fold_channel_biases():
                dve.wait_ge(nat_kf_in, 16)
                for m in range(NH):
                    ins = v.scalar_tensor_tensor(junk, nat_kf[:, m, :], 1.0, ln2b_all, ALU.mult, ALU.mult,
                                                 accum_out=bias_kf[:, m:m + 1])
                    if m < NH - 1:
                        after(ins)
                ins.then_inc(bias_ready, 1)

            def spread_ln2_b():
                step(v.tensor_copy(ln2b_rep[:, 0, :], vec_cols[:, 0, 4:5].to_broadcast([P, P])))
                step(v.memset(ln2b_rep[0:64, 1, :], 0.0))
                v.tensor_copy(ln2b_rep[64:128, 1, :], vec_cols[64:128, 1, 4:5].to_broadcast([64, P]))\
                    .then_inc(bias_ready, 1)

            set_up()
            set_edges()
            embed_statistics(0, 0)
            prepare(0, 1)
            embed_normalise(0, 0)
            prepare(1, 3)
            embed_statistics(0, 1)
            split_low("qkv", 0, 0)
            dve.wait_ge(lnb_in, 32)
            dve.wait_ge(nat_qkv_in, 16 * 7)
            for m in range(QKV):
                fold_bias(bias_qkv, nat_qkv, ln1b_all, m)
            v.tensor_scalar(bias_half[:], bias_qkv[:], 0.5, None, ALU.mult).then_inc(bias_ready, 1)
            embed_normalise(0, 1)
            prepare(3, 5)
            maxima(0, 0)
            split_low("qkv", 0, 1)
            common_max(0, 0)
            scans(0, 0)
            prepare(5, 7)
            embed_statistics(1, 0)
            maxima(0, 2)
            sums(0, 0)
            embed_normalise(1, 0)
            embed_statistics(1, 1)
            common_max(0, 2)
            split_low("qkv", 1, 0)
            prepare(7, 9)
            embed_normalise(1, 1)
            scans(0, 2)
            gated(0, 0)
            maxima(0, 1)
            split_low("qkv", 1, 1)
            sums(0, 2)
            spread_ln2_b()
            prepare(9, len(prep) - 1)
            common_max(0, 1)
            prepare(len(prep) - 1, len(prep))
            gated(0, 2)
            dve.wait_ge(prep_high, len(prep) + 1)
            v.tensor_tensor(rf_bias[32:33, :], prep_bank(len(prep))[32:33, 0:C],
                            rf_bias_h[32:33, :], ALU.subtract).then_inc(prep_low, 1)
            scans(0, 1)
            embed_statistics(2, 0)
            embed_statistics(2, 1)
            embed_normalise(2, 0)
            embed_normalise(2, 1)
            add_attention(0, 0)
            split_low("qkv", 2, 0)
            sums(0, 1)
            fold_channel_biases()
            gated(0, 1)
            normalise("mix", 0, 0, resid[:, 0])
            for s in range(1, PAIRS + 1):
                mix, wkv, prj, nxt = s - 1, s, s + 1, s + 2
                if has(prj):
                    split_low("qkv", prj, 1)
                else:
                    split_low("mix", mix, 0)
                if has(wkv):
                    maxima(wkv, 0)
                add_attention(mix, 1)
                if has(wkv):
                    common_max(wkv, 0)
                if has(prj):
                    split_low("mix", mix, 0)
                normalise("mix", mix, 1, resid[:, 1])
                if has(wkv):
                    scans(wkv, 0)
                if not has(prj):
                    split_low("mix", mix, 1)
                if has(wkv):
                    maxima(wkv, 2)
                if has(prj):
                    split_low("mix", mix, 1)
                if has(wkv):
                    sums(wkv, 0)
                    common_max(wkv, 2)
                square(mix, 0)
                if has(wkv):
                    scans(wkv, 2)
                    gated(wkv, 0)
                    maxima(wkv, 1)
                square(mix, 1)
                add_channel_mix(mix, 0)
                if has(wkv):
                    sums(wkv, 2)
                normalise("ffn", mix, 0, resid[:, 0])
                if has(wkv):
                    common_max(wkv, 1)
                split_low("ffn", mix, 0)
                add_channel_mix(mix, 1)
                if has(wkv):
                    scans(wkv, 1)
                normalise("ffn", mix, 1, resid[:, 1])
                if has(wkv):
                    gated(wkv, 2)
                    sums(wkv, 1)
                split_low("ffn", mix, 1)
                if has(nxt):
                    embed_statistics(nxt, 0)
                add_ffn(mix, 0)
                if has(nxt):
                    embed_statistics(nxt, 1)
                    embed_normalise(nxt, 0)
                    embed_normalise(nxt, 1)
                if has(wkv):
                    gated(wkv, 1)
                    add_attention(wkv, 0)
                if has(nxt):
                    split_low("qkv", nxt, 0)
                if has(wkv):
                    normalise("mix", wkv, 0, resid[:, 0])
                add_ffn(mix, 1)

        @block.tensor
        def _(pe):
            mm = nc.tensor.matmul

            def turn(dst, src, rows_in):
                return nc.tensor.transpose(dst, src, ident[0:rows_in, 0:rows_in])

            def prepare(first_item, last_item):
                for n, (kind, dst, nat, m, sizes, ln) in list(enumerate(prep))[first_item:last_item]:
                    bank = prep_bank(n)
                    if kind == "split":
                        sem_in = SPLIT_W[id(dst)]
                        pe.wait_ge(sem_in, 16 * 7 if sem_in is nat_qkv_in else 16)
                    else:
                        pe.wait_ge({"wo": nat_wo_in, "rf": nat_rf_in, "vf": nat_vf_in}[kind], 32)
                    if n >= 5:
                        pe.wait_ge(prep_high, n - 1)
                        pe.wait_ge(prep_low, splits(n - 1))
                    at = 0
                    if kind == "vf":
                        for i in range(2):
                            c = slice((m + i) * P, (m + i + 1) * P)
                            turn(bank[:, i * C:i * C + P], nat[:, 0, c], P)
                            ins = turn(bank[:, i * C + P:i * C + C], nat[0:CB, 1, c], CB)
                    else:
                        for i, size in enumerate(sizes):
                            turn(bank[:, at:at + size], nat[0:size, m + i, 0:P], size)
                            ins = turn(bank[:, 256 + at:256 + at + size], nat[0:size, m + i, C - P:C], size)
                            at += size
                    ins.then_inc(prep_filled, 1)

            def transposes(kind, p, q):
                e = norm_no[kind, p, q]
                pe.wait_ge(normed_ready, e + 1)
                if e:
                    pe.wait_ge(low_ready, 2 * e)
                for j in range(NT):
                    cols = slice(j, T, NT) if kind == "qkv" else slice(j * P, (j + 1) * P)
                    turn(ps_t[:, 0, cols], normed[:, e % 2, j, 0:P], P)
                    ins = turn(ps_t[:, 1, cols], normed[:, e % 2, j, C - P:C], P)
                ins.then_inc(t_filled, 1)

            def project(kind, p, q, w, chunks):
                e = norm_no[kind, p, q]
                n = chunk_start(kind, p, q)
                pe.wait_ge(low_ready, 2 * e + 2)
                high, low, b = act_a[:, e % 2, 0, :], act_a[:, e % 2, 1, :], act_b[:, e % 2, :]
                for m in range(chunks):
                    if n + m >= RING:
                        pe.wait_ge(c_freed, n + m + 1 - RING)
                    o, c = ps_c[:, (n + m) % RING], slice(m * P, (m + 1) * P)
                    mm(o, w[:, 0, c], high, start=True, stop=False)
                    mm(o, w[:, 1, c], high, start=False, stop=False)
                    mm(o, w[:, 0, c], low, start=False, stop=False)
                    mm(o, w[:, 2, c], b, start=False, stop=False)
                    mm(o, w[:, 3, c], b, start=False, stop=True).then_inc(c_filled, 1)

            def gate_rows(p, q):
                e = norm_no["mix", p, q]
                n = chunk_start("mix", p, q) + NH
                for h in range(2):
                    pe.wait_ge(c_freed, n + h + 1 - RING)
                    for i in range(2):
                        tok = slice((2 * h + i) * P, (2 * h + i + 1) * P)
                        o = ps_c[:, (n + h) % RING, i * C:(i + 1) * C]
                        high, low, b = act_a[:, e % 2, 0, tok], act_a[:, e % 2, 1, tok], act_b[:, e % 2, tok]
                        mm(o, high, rf_w[:, 0, :], start=True, stop=False)
                        mm(o, high, rf_w[:, 1, :], start=False, stop=False)
                        mm(o, low, rf_w[:, 0, :], start=False, stop=False)
                        mm(o, b, rf_w[:, 2, :], start=False, stop=False)
                        mm(o, b, rf_w[:, 3, :], start=False, stop=False)
                        ins = mm(o, rf_pick[:], rf_bias[:], start=False, stop=True)
                    ins.then_inc(c_filled, 1)

            def attention_out(p, q):
                n = out_no["attn", p, q]
                pe.wait_ge(z_ready, tile_no(p, 1 if q else 2) + 1)
                for h in range(2):
                    if n + h >= 2:
                        pe.wait_ge(o_freed, n + h - 1)
                    for i in range(2):
                        o, tok = ps_o[:, h, i * C:(i + 1) * C], slice(2 * h + i, T, NT)
                        mm(o, mixed[:, q, tok], wo_a[:], start=True, stop=False)
                        ins = mm(o, mixed[:, 2, tok], wo_b[:, q, :], start=False, stop=True)
                    ins.then_inc(o_filled, 1)

            def hidden_out(kind, p, q, w, tiles, chunk_ready):
                n = out_no[kind, p, q]
                for j in tiles:
                    h, i = divmod(j, 2)
                    if i == 0:
                        pe.wait_ge(o_freed, n + h - 1)
                    o = ps_o[:, h, i * C:(i + 1) * C]
                    for m in range(NH):
                        if j == 0:
                            pe.wait_ge(*chunk_ready(m))
                        ins = mm(o, hid[:, q, m, j * P:(j + 1) * P], w[:, m, :],
                                 start=(m == 0), stop=(m == NH - 1))
                    if i == 1:
                        ins.then_inc(o_filled, 1)

            def channel_out(p, q, tiles=range(NT)):
                hidden_out("chan", p, q, vf_w, tiles, lambda m: (odd_ready if m % 2 else even_ready,
                                                                 (2 * p + q) * NH // 2 + m // 2 + 1))

            def ffn_out(p, q):
                hidden_out("ffn", p, q, out_w, range(NT),
                           lambda m: (c_freed, chunk_start("ffn", p, q) + m + 1))

            pe.wait_ge(consts, 1)
            pe.wait_ge(vecs_in, 16 * 6)
            turn(ps_c[:, 0, 0:5 + NH], vec_rows[:, 0:P], 5 + NH)
            turn(ps_c[:, 0, 16:21], vec_rows[0:5, C - P:C], 5).then_inc(prep_filled, 1)
            prepare(0, 5)
            transposes("qkv", 0, 0)
            pe.wait_ge(prep_low, splits(3))
            project("qkv", 0, 0, qkv_w, QKV)
            transposes("qkv", 0, 1)
            prepare(5, 7)
            project("qkv", 0, 1, qkv_w, QKV)
            prepare(7, 9)
            transposes("qkv", 1, 0)
            project("qkv", 1, 0, qkv_w, QKV)
            prepare(9, 11)
            transposes("qkv", 1, 1)
            prepare(11, len(prep) - 1)
            project("qkv", 1, 1, qkv_w, QKV)
            prepare(len(prep) - 1, len(prep))
            pe.wait_ge(bias_ready, 2)
            pe.wait_ge(prep_high, len(prep))
            pe.wait_ge(prep_low, splits(len(prep) - 1))
            o = prep_bank(len(prep))[:, 0:C]
            mm(o, ln2b_rep[:, 0, :], nat_rf_t[:, 0, :], start=True, stop=False)
            mm(o, ln2b_rep[:, 1, :], nat_rf_t[:, 1, :], start=False, stop=True).then_inc(prep_filled, 1)
            pe.wait_ge(prep_low, splits(len(prep)) + 1)
            pe.wait_ge(out_w_in, 16)
            attention_out(0, 0)
            transposes("qkv", 2, 0)
            for s in range(1, PAIRS + 1):
                mix, wkv, prj, nxt = s - 1, s, s + 1, s + 2
                if has(prj):
                    transposes("qkv", prj, 1)
                if has(prj) and mix > 0:
                    attention_out(mix, 1)
                if has(prj):
                    project("qkv", prj, 0, qkv_w, QKV)
                if mix == 0:
                    attention_out(mix, 1)
                transposes("mix", mix, 0)
                if not has(prj):
                    attention_out(mix, 1)
                if has(prj):
                    project("qkv", prj, 1, qkv_w, QKV)
                    transposes("mix", mix, 1)
                if mix == 0:
                    pe.wait_ge(mix_halves_in, 16 * 2)
                project("mix", mix, 0, kf_w, NH)
                if not has(prj):
                    transposes("mix", mix, 1)
                gate_rows(mix, 0)
                project("mix", mix, 1, kf_w, NH)
                channel_out(mix, 0)
                gate_rows(mix, 1)
                channel_out(mix, 1, range(NT - 1))
                transposes("ffn", mix, 0)
                channel_out(mix, 1, [NT - 1])
                if mix == 0:
                    pe.wait_ge(ffn_halves_in, 16)
                project("ffn", mix, 0, in_w, NH)
                transposes("ffn", mix, 1)
                ffn_out(mix, 0)
                project("ffn", mix, 1, in_w, NH)
                if has(wkv):
                    attention_out(wkv, 0)
                if has(nxt):
                    transposes("qkv", nxt, 0)
                ffn_out(mix, 1)


_INS = ["x", "L0_tok_weight", "L0_attn_ln1_w", "L0_attn_ln1_b", "L0_attn_ln2_w", "L0_attn_ln2_b",
        "L0_attn_decay", "L0_attn_first", "L0_attn_Wk_a", "L0_attn_Wv_a", "L0_attn_Wr_a", "L0_attn_Wo_a",
        "L0_attn_Wk_f", "L0_attn_Wv_f", "L0_attn_Wr_f", "L0_ffn_in_weight", "L0_ffn_in_bias",
        "L0_ffn_out_weight"]


def kernel(**inputs):
    import numpy as _np
    import concourse.bacc as _bacc
    from concourse import mybir as _mybir
    from concourse.bass_utils import run_bass_kernel_spmd as _run

    nc = _bacc.Bacc("TRN2", target_bir_lowering=False, num_devices=1)
    arrays, args = {}, []
    for name in _INS:
        a = _np.ascontiguousarray(inputs[name])
        arrays[f"in_{name}"] = a
        args.append(nc.dram_tensor(f"in_{name}", a.shape, _mybir.dt.from_np(a.dtype), kind="ExternalInput").ap())
    shape = tuple(inputs["x"].shape) + (inputs["L0_tok_weight"].shape[1],)
    out = nc.dram_tensor("out", shape, _mybir.dt.float32, kind="ExternalOutput").ap()
    tower(nc, *args, out)
    r = _run(nc, [arrays], core_ids=[0])
    return r.results[0]["out"]
```
